# Optimizing a Trainium2 kernel written in Bass

```python
import numpy as np
import jax
import jax.numpy as jnp

def _softmax(x, axis=-1):
    return jax.nn.softmax(x, axis=axis)

def _gelu(x):
    return jax.nn.gelu(x, approximate=True)

def _silu(x):
    return jax.nn.silu(x)

def _sigmoid(x):
    return jax.nn.sigmoid(x)

def _layernorm(x, axis=-1, eps=1e-05):
    m = jnp.mean(x, axis=axis, keepdims=True)
    v = jnp.var(x, axis=axis, keepdims=True)
    return (x - m) / jnp.sqrt(v + eps)

def _scatter_add(tgt, idx, src, axis=0):
    return tgt.at[idx].add(src)

def _segment_sum(src, seg, n):
    return jax.ops.segment_sum(src, seg, n)
kernel_name = 'mk_prb_d2_jaxref_r8_a083d4'

def setup_inputs(seed: int=0):
    np.random.seed(seed)
    _w = jnp.asarray

    def _L0_attn_setup():
        import math
        import jax, jax.numpy as jnp
        import numpy as np
        NUM_HEADS = 32
        HIDDEN = 512
        HEAD_DIM = HIDDEN // NUM_HEADS
        NEG_INF = -1e+30

        def _alibi_slopes(n: int) -> jnp.ndarray:
            cp2 = 2 ** math.floor(math.log2(n))
            base = 2.0 ** (-2.0 ** (-(math.log2(cp2) - 3)))
            slopes = base ** np.arange(1, cp2 + 1, dtype=np.float64)
            if cp2 != n:
                extra_base = 2.0 ** (-2.0 ** (-(math.log2(2 * cp2) - 3)))
                rem = min(cp2, n - cp2)
                extra = extra_base ** np.arange(1, 1 + 2 * rem, 2, dtype=np.float64)
                slopes = np.concatenate([slopes, extra])
            return jnp.asarray(slopes, dtype=jnp.float32)
        key = jax.random.key(seed)
        k1, k2, k3 = jax.random.split(key, 3)
        B, S = (2, 256)
        hidden_states = jax.random.normal(k1, (B, S, HIDDEN), dtype=jnp.float32)
        Wqkv = jax.random.normal(k2, (HIDDEN, NUM_HEADS * HEAD_DIM + 2 * HEAD_DIM), dtype=jnp.float32) * 0.02
        Wo = jax.random.normal(k3, (HIDDEN, HIDDEN), dtype=jnp.float32) * 0.02
        return {'hidden_states': hidden_states, 'Wqkv': Wqkv, 'Wo': Wo}
    _L0_attn_in = _L0_attn_setup()

    def _L0_ffn_setup():
        import jax, jax.numpy as jnp
        import numpy as np
        LORA_R = 16
        SCALE = 16.0 / np.sqrt(16.0)
        NUM_EXPERTS = 4
        TOP_K = 2
        IN_F = 512
        OUT_F = 512
        key = jax.random.key(seed)
        k_x, k_a, k_b, k_r = jax.random.split(key, 4)
        x = jax.random.normal(k_x, (2, 256, IN_F), dtype=jnp.float32)
        A = jax.random.normal(k_a, (NUM_EXPERTS, LORA_R, IN_F), dtype=jnp.float32) * (1.0 / np.sqrt(IN_F))
        B = jax.random.normal(k_b, (NUM_EXPERTS, OUT_F, LORA_R), dtype=jnp.float32) * 0.02
        Wr = jax.random.normal(k_r, (NUM_EXPERTS, IN_F), dtype=jnp.float32) * 0.02
        return {'x': x, 'A': A, 'B': B, 'Wr': Wr}
    _L0_ffn_in = _L0_ffn_setup()

    def _L1_attn_setup():
        import jax, jax.numpy as jnp
        import numpy as np
        EMB_DIM = 512
        N_HEADS = 32
        QKV_DIM = EMB_DIM // N_HEADS
        B, S = (4, 512)
        key = jax.random.key(seed)
        ks = jax.random.split(key, 7)
        std = 1.0 / np.sqrt(EMB_DIM)
        x = jax.random.normal(ks[0], (B, S, EMB_DIM), dtype=jnp.float32)
        Wq = jax.random.normal(ks[1], (EMB_DIM, QKV_DIM, N_HEADS), dtype=jnp.float32) * std
        bq = jnp.zeros((QKV_DIM, N_HEADS), dtype=jnp.float32)
        Wk = jax.random.normal(ks[2], (EMB_DIM, QKV_DIM, 1), dtype=jnp.float32) * std
        bk = jnp.zeros((QKV_DIM, 1), dtype=jnp.float32)
        Wv = jax.random.normal(ks[3], (EMB_DIM, QKV_DIM, 1), dtype=jnp.float32) * std
        bv = jnp.zeros((QKV_DIM, 1), dtype=jnp.float32)
        return {'x': x, 'Wq': Wq, 'bq': bq, 'Wk': Wk, 'bk': bk, 'Wv': Wv, 'bv': bv}
    _L1_attn_in = _L1_attn_setup()

    def _L1_ffn_setup():
        import jax, jax.numpy as jnp
        import numpy as np

        def _dequant_linear(x, wq, scale):
            w = wq.astype(jnp.float32) * scale[:, None]
            return jnp.einsum('bsh,oh->bso', x, w)
        key = jax.random.key(seed)
        ks = jax.random.split(key, 7)
        B, S, H, I = (2, 256, 512, 1792)
        x = jax.random.normal(ks[0], (B, S, H), dtype=jnp.float32)
        gate_wq = jax.random.randint(ks[1], (I, H), -128, 128, dtype=jnp.int32)
        up_wq = jax.random.randint(ks[2], (I, H), -128, 128, dtype=jnp.int32)
        down_wq = jax.random.randint(ks[3], (H, I), -128, 128, dtype=jnp.int32)
        gate_scale = jax.random.uniform(ks[4], (I,), dtype=jnp.float32, minval=0.5, maxval=1.5) / (127.0 * np.sqrt(H))
        up_scale = jax.random.uniform(ks[5], (I,), dtype=jnp.float32, minval=0.5, maxval=1.5) / (127.0 * np.sqrt(H))
        down_scale = jax.random.uniform(ks[6], (H,), dtype=jnp.float32, minval=0.5, maxval=1.5) / (127.0 * np.sqrt(I))
        return {'x': x, 'gate_wq': gate_wq, 'gate_scale': gate_scale, 'up_wq': up_wq, 'up_scale': up_scale, 'down_wq': down_wq, 'down_scale': down_scale}
    _L1_ffn_in = _L1_ffn_setup()
    _d = {'L0_attn_hidden_states': _L0_attn_in['hidden_states'], 'L0_attn_Wqkv': _L0_attn_in['Wqkv'], 'L0_attn_Wo': _L0_attn_in['Wo'], 'L0_ffn_A': _L0_ffn_in['A'], 'L0_ffn_B': _L0_ffn_in['B'], 'L0_ffn_Wr': _L0_ffn_in['Wr'], 'L1_attn_Wq': _L1_attn_in['Wq'], 'L1_attn_bq': _L1_attn_in['bq'], 'L1_attn_Wk': _L1_attn_in['Wk'], 'L1_attn_bk': _L1_attn_in['bk'], 'L1_attn_Wv': _L1_attn_in['Wv'], 'L1_attn_bv': _L1_attn_in['bv'], 'L1_ffn_gate_wq': _L1_ffn_in['gate_wq'], 'L1_ffn_gate_scale': _L1_ffn_in['gate_scale'], 'L1_ffn_up_wq': _L1_ffn_in['up_wq'], 'L1_ffn_up_scale': _L1_ffn_in['up_scale'], 'L1_ffn_down_wq': _L1_ffn_in['down_wq'], 'L1_ffn_down_scale': _L1_ffn_in['down_scale']}
    _x0 = _d['L0_attn_hidden_states']
    _d['L0_attn_hidden_states'] = jax.random.normal(jax.random.fold_in(jax.random.key(seed), 1), (8, 256, 512), dtype=_x0.dtype)
    del _x0
    return _d

def reference(L0_attn_hidden_states, L0_attn_Wqkv, L0_attn_Wo, L0_ffn_A, L0_ffn_B, L0_ffn_Wr, L1_attn_Wq, L1_attn_bq, L1_attn_Wk, L1_attn_bk, L1_attn_Wv, L1_attn_bv, L1_ffn_gate_wq, L1_ffn_gate_scale, L1_ffn_up_wq, L1_ffn_up_scale, L1_ffn_down_wq, L1_ffn_down_scale):

    def _L0_attn_ref(hidden_states, Wqkv, Wo):
        import math
        import jax, jax.numpy as jnp
        import numpy as np
        NUM_HEADS = 32
        HIDDEN = 512
        HEAD_DIM = HIDDEN // NUM_HEADS
        NEG_INF = -1e+30

        def _alibi_slopes(n: int) -> jnp.ndarray:
            cp2 = 2 ** math.floor(math.log2(n))
            base = 2.0 ** (-2.0 ** (-(math.log2(cp2) - 3)))
            slopes = base ** np.arange(1, cp2 + 1, dtype=np.float64)
            if cp2 != n:
                extra_base = 2.0 ** (-2.0 ** (-(math.log2(2 * cp2) - 3)))
                rem = min(cp2, n - cp2)
                extra = extra_base ** np.arange(1, 1 + 2 * rem, 2, dtype=np.float64)
                slopes = np.concatenate([slopes, extra])
            return jnp.asarray(slopes, dtype=jnp.float32)
        B, S, H = hidden_states.shape
        nH, d = (NUM_HEADS, HEAD_DIM)
        scale = d ** (-0.5)
        qkv = hidden_states @ Wqkv
        q = qkv[..., :nH * d].reshape(B, S, nH, d)
        k = qkv[..., nH * d:nH * d + d]
        v = qkv[..., nH * d + d:]
        scores = jnp.einsum('bqhd,bkd->bhqk', q, k) * scale
        pos_q = jnp.arange(S)[:, None]
        pos_k = jnp.arange(S)[None, :]
        slopes = _alibi_slopes(nH)
        alibi = slopes[:, None, None] * (pos_k - pos_q).astype(jnp.float32)
        causal = pos_k <= pos_q
        scores = jnp.where(causal[None, None], scores + alibi[None], NEG_INF)
        probs = jax.nn.softmax(scores, axis=-1)
        attn = jnp.einsum('bhqk,bkd->bqhd', probs, v).reshape(B, S, H)
        return attn @ Wo

    def _L0_ffn_ref(x, A, B, Wr):
        import jax, jax.numpy as jnp
        import numpy as np
        LORA_R = 16
        SCALE = 16.0 / np.sqrt(16.0)
        NUM_EXPERTS = 4
        TOP_K = 2
        IN_F = 512
        OUT_F = 512
        orig_shape = x.shape
        flat = x.reshape(-1, orig_shape[-1])
        logits = flat @ Wr.T
        topk_vals, topk_idx = jax.lax.top_k(logits, TOP_K)
        T = flat.shape[0]
        neg_inf = jnp.finfo(logits.dtype).min
        sparse = jnp.full_like(logits, neg_inf)
        rows = jnp.arange(T)[:, None]
        sparse = sparse.at[rows, topk_idx].set(topk_vals)
        gates = jax.nn.softmax(sparse, axis=-1)
        mid = jnp.einsum('tf,erf->ter', flat, A)
        all_deltas = jnp.einsum('ter,eor->teo', mid, B) * SCALE
        delta = jnp.sum(gates[:, :, None] * all_deltas, axis=1)
        return delta.reshape(*orig_shape[:-1], -1)

    def _L1_attn_ref(x, Wq, bq, Wk, bk, Wv, bv):
        import jax, jax.numpy as jnp
        import numpy as np
        EMB_DIM = 512
        N_HEADS = 32
        QKV_DIM = EMB_DIM // N_HEADS
        B, S = (4, 512)
        q = jnp.einsum('bsD,Ddh->bsdh', x, Wq) + bq
        k = (jnp.einsum('bsD,Ddh->bsdh', x, Wk) + bk)[..., 0]
        v = (jnp.einsum('bsD,Ddh->bsdh', x, Wv) + bv)[..., 0]
        qkv_dim = q.shape[-2]
        n_heads = q.shape[-1]
        scale = 1.0 / jnp.sqrt(jnp.asarray(qkv_dim, dtype=q.dtype))
        scores = jnp.einsum('bsdh,bse->bsde', q, k) * scale
        p = jax.nn.softmax(scores, axis=-1)
        o = jnp.einsum('bsde,bse->bsd', p, v)
        out = jnp.broadcast_to(o[..., None], o.shape + (n_heads,))
        return out.reshape(x.shape[:-1] + (qkv_dim * n_heads,))

    def _L1_ffn_ref(x, gate_wq, gate_scale, up_wq, up_scale, down_wq, down_scale):
        import jax, jax.numpy as jnp
        import numpy as np

        def _dequant_linear(x, wq, scale):
            w = wq.astype(jnp.float32) * scale[:, None]
            return jnp.einsum('bsh,oh->bso', x, w)
        gate = _dequant_linear(x, gate_wq, gate_scale)
        up = _dequant_linear(x, up_wq, up_scale)
        h = jax.nn.silu(gate) * up
        return _dequant_linear(h, down_wq, down_scale)
    x = L0_attn_hidden_states
    xn = _layernorm(x, axis=-1)
    x = x + _L0_attn_ref(xn, L0_attn_Wqkv, L0_attn_Wo) + _L0_ffn_ref(xn, L0_ffn_A, L0_ffn_B, L0_ffn_Wr)
    xn = _layernorm(x, axis=-1)
    x = x + _L1_attn_ref(xn, L1_attn_Wq, L1_attn_bq, L1_attn_Wk, L1_attn_bk, L1_attn_Wv, L1_attn_bv) + _L1_ffn_ref(xn, L1_ffn_gate_wq, L1_ffn_gate_scale, L1_ffn_up_wq, L1_ffn_up_scale, L1_ffn_down_wq, L1_ffn_down_scale)
    return x

_drawn_inputs = setup_inputs


def setup_inputs(seed=0):
    import zlib

    import numpy as np

    out = dict(_drawn_inputs(seed))
    spreads = {'L1_attn_bq': (0.0, 0.1), 'L1_attn_bk': (0.0, 0.1), 'L1_attn_bv': (0.0, 0.1)}
    factors = {}
    for name, (base, spread) in spreads.items():
        noise = np.random.default_rng([zlib.crc32(name.encode()), seed]).standard_normal(out[name].shape)
        drawn = base * np.exp(spread * noise) if base else spread * noise
        out[name] = jnp.asarray(drawn.astype(out[name].dtype))
    for name, factor in factors.items():
        out[name] = (out[name] * factor).astype(out[name].dtype)
    return out
```

```python
import math
from contextlib import ExitStack

import numpy as np
import concourse.bass as bass
from concourse import mybir

P = 128
BATCH, SEQ, HID = 8, 256, 512
NH, HD = 32, 16
CHUNK = 512
NCH = BATCH * SEQ // CHUNK
NT = CHUNK // P
NK = HID // P
NB = CHUNK // SEQ
HG = 4
NHG = NH // HG
NE, LR = 4, 16
INTER = 1792
NI = INTER // P
EPS = 1e-5
SCALE = HD ** -0.5
LORA_SCALE = 16.0 / math.sqrt(16.0)

PART_Q = [0, 0, 1, 0, 2, 1]
PART_K = [0, 1, 0, 2, 0, 1]
R_ALIBI = 6 * HD
R_MAX = R_ALIBI + 6
R_BLOCK = R_MAX + 3
MB = 8
ROWS = R_BLOCK + P // MB - 1

TOKC = 2 * HD + NE + NE * LR
C_V, C_L, C_M = HD, 2 * HD, 2 * HD + NE
C1 = 3 * HD
XS = 256.0
HS = 2.0 ** -17

U_XT, U_TOK, U_KT, U_Q, U_NM0, U_PV0, U_NM1, U_PV1, U_AT, U_OUT = 0, 4, 10, 6, 11, 12, 16, 17, 21, 26
UA = 30
F0 = [k * P for k in range(NK)] + [HID + NE * LR - P]
V_XT, V_TOK, V_GU, V_DOWN = 0, 4, 6, 6 + 2 * NI
UB = V_DOWN + NT
NSTAGE = 4
SU = 3 * NHG

F32, BF16, F16, I32 = mybir.dt.float32, mybir.dt.bfloat16, mybir.dt.float16, mybir.dt.int32
ALU = mybir.AluOpType
ACT = mybir.ActivationFunctionType
AX = mybir.AxisListType

STAGE_A = ([("a_ln",), ("a_xT",), ("a_tok",), ("a_q",), ("a_kT",), ("a_gate",)]
           + [("a_max", 0, g) for g in range(NHG)] + [("a_nm", 0)]
           + [s for g in range(NHG) for s in
              ([("a_max", 1, g), ("a_exp", 0, g)] + ([("a_pv", 0, g - 1)] if g else []))]
           + [("a_nm", 1), ("a_pv", 0, NHG - 1)]
           + [s for g in range(NHG) for s in ([("a_exp", 1, g)] + ([("a_pv", 1, g - 1)] if g else []))]
           + [("a_pv", 1, NHG - 1), ("a_attT",), ("a_out",)])
STAGE_B = ([("b_ln",), ("b_xT",), ("b_tok",), ("b_att",)]
           + [("b_gu", i) for i in range(NI)] + [("b_down", t) for t in range(NT)])


def interleave(a, b):
    out, n = [], 0
    for i, step in enumerate(a):
        while n < len(b) and n * (len(a) - 1) <= i * len(b):
            out.append(b[n])
            n += 1
        if i == len(a) - 1:
            out += b[n:]
        out.append(step)
    return out


def build(nc, x, wqkv, wo, lora_a, lora_b, wr, wq1, bq1, wk1, bk1, wv1, bv1,
          gate_w, gate_s, up_w, up_s, down_w, down_s, q_rows, q_blocks, k_cols, mask, ident_f, ident_b, tri, out):
    with ExitStack() as ctx:
        def sb(name, shape, dt):
            return ctx.enter_context(nc.sbuf_tensor(name, shape, dt))

        def sem(name):
            return ctx.enter_context(nc.semaphore(name))

        identf = sb("identf", [P, P], F32)
        identb = sb("identb", [P, P], BF16)
        maskb = sb("maskb", [P, P], BF16)
        tri_sb = sb("tri_sb", [P, NE, NE], F32)
        wq_sb = sb("wq_sb", [P, NK, HID], F32)
        wtok = sb("wtok", [P, NK, TOKC], F32)
        wo_sb = sb("wo_sb", [P, NK + 1, HID], F32)
        w48f = sb("w48f", [P, NK, C1], F32)
        w48r = sb("w48r", [P, NK, C1], F32)
        w48 = sb("w48", [P, NK, 3, C1], BF16)
        bias48 = sb("bias48", [P, C1], F32)
        wgu = sb("wgu", [P, 2, NK, INTER], F16)
        wd = sb("wd", [P, NI, HID], F16)
        sg = sb("sg", [P, NI], F32)
        su = sb("su", [P, NI], F32)
        sg_neg = sb("sg_neg", [P, NI], F32)
        sgx = sb("sgx", [P, NI], F32)
        sux = sb("sux", [P, NI], F32)
        sprod = sb("sprod", [P, NI], F32)
        cmax = sb("cmax", [P, 4], F32)
        dsb = sb("dsb", [P, HID], F32)
        x_sb = sb("x_sb", [P, NT, HID], F32)
        attn = sb("attn", [P, NT, HID + NE * LR], F32)
        xn0 = attn[:, :, 0:HID]
        st0 = sb("st0", [P, NT, 6], F32)
        mv0 = sb("mv0", [P, NT, 2], F32)
        rs0 = sb("rs0", [P, NT], F32)
        mhalf = sb("mhalf", [P, NT], F32)
        qparts = sb("qparts", [P, 3 * NK * CHUNK], BF16)
        qs = qparts[:, :].rearrange("p (a m t) -> p a m t", a=3, m=NK)
        attnT = qparts[:, 0:5 * CHUNK * 2].bitcast(F32).rearrange("p (k t) -> p k t", k=5)
        rq = sb("rq", [P, 2, CHUNK], F32)
        probs = sb("probs", [P, 2, 3, CHUNK], F32)
        xT = probs[:, :, :, :].rearrange("p s u t -> p (s u) t")[:, 0:NK, :]
        kc = sb("kc", [P, NT, ROWS], BF16)
        kres = sb("kres", [P, NT, HD], F32)
        kk = sb("kk", [ROWS, NT, P], BF16)
        vv = sb("vv", [P, NT, HD + 1], F32)
        qq = sb("qq", [ROWS, NH, CHUNK], BF16)
        mx = sb("mx", [P, NT, NH], F32)
        nres = sb("nres", [P, 2, NH], F32)
        nmp = sb("nmp", [P, NB, 2, 3, NH], BF16)
        nmT = sb("nmT", [3 * NH, NB, SEQ], BF16)
        rden = sb("rden", [P, 2, 2 * HG], F32)
        lm = sb("lm", [P, NT, NE + NE * LR], F32)
        gate = sb("gate", [P, NT, NE], F32)
        gsum = sb("gsum", [P, NT], F32)
        gmx = sb("gmx", [P, NT], F32)
        gex = sb("gex", [P, NT, NE], F32)
        gcmp = sb("gcmp", [P, NT, NE, NE], F32)
        geq = sb("geq", [P, NT, NE, NE], F32)
        grk = sb("grk", [P, NT, NE], F32)
        x1 = sb("x1", [P, NT, HID], F32)
        st1 = sb("st1", [P, NT, 6], F32)
        mv1 = sb("mv1", [P, NT, 2], F32)
        rs1 = sb("rs1", [P, NT], F32)
        hbuf = sb("hbuf", [P, 2, NI, CHUNK], F16)
        hflat = hbuf[:, :, :, :].rearrange("p a i t -> p (a i t)")
        xn1 = hflat[:, 0:NT * HID * 2].bitcast(F32).rearrange("p (t h) -> p t h", t=NT)
        S = hflat[:, NT * HID * 2:NT * (HID + HD * HD) * 2].bitcast(F32).rearrange(
            "p (t d e) -> p t d e", t=NT, d=HD)
        stage = [hflat[:, s * INTER * 2:(s + 1) * INTER * 2].bitcast(I32) for s in range(NSTAGE)]
        xs = sb("xs", [P, 2, NK, CHUNK], F16)
        wq1_st = xs[:, :, :, :].rearrange("p a k t -> p (a k t)").bitcast(F32).rearrange(
            "p (k d h) -> p k d h", k=NK, h=NH)
        t48 = sb("t48", [P, NT, C1], F32)
        kext = sb("kext", [P, 2, NT], F32)
        m1 = sb("m1", [P, 2, NT, HD], F32)
        den1 = sb("den1", [P, NT, HD], F32)
        o1 = sb("o1", [P, NT, HD], F32)
        ebuf = sb("ebuf", [P, 2, CHUNK], F32)
        hf = sb("hf", [P, 2, CHUNK], F32)
        ytmp = sb("ytmp", [P, HID], F32)
        bq_st = ytmp[:, :].rearrange("p (d h) -> p d h", h=NH)

        def bank(name, dt=F32, n=512):
            return ctx.enter_context(nc.psum_tensor(name, [P, n], dt))

        ab = [bank("a_bank0"), bank("a_bank1")]
        bb = [bank("b_bank0"), bank("b_bank1")]
        mb = [bank("max_bank0"), bank("max_bank1")]
        eb = [bank("exp_bank0"), bank("exp_bank1")]

        s_const, s_w, s_w1 = sem("constants_loaded"), sem("weights_loaded"), sem("layer1_small_loaded")
        s_init = sem("pool_constants_set")
        s_stage = [sem(f"stage{i}_loaded") for i in range(NSTAGE)]
        s_conv = sem("ffn_weights_converted")
        s_cmax, s_call, s_wprep = sem("scale_product_ready"), sem("scale_maximum_ready"), sem("layer1_operands_ready")
        s_x = sem("x_loaded")
        s_var0, s_eps0, s_rs0, s_xn0 = sem("variance0"), sem("variance0_plus_eps"), sem("rstd0"), sem("xn0_ready")
        s_var1, s_eps1, s_rs1, s_xn1 = sem("variance1"), sem("variance1_plus_eps"), sem("rstd1"), sem("xn1_ready")
        a_full = [sem("a_bank0_full"), sem("a_bank1_full")]
        a_free = [sem("a_bank0_used"), sem("a_bank1_used")]
        b_full = [sem("b_bank0_full"), sem("b_bank1_full")]
        b_free = [sem("b_bank0_used"), sem("b_bank1_used")]
        m_full = [sem("max_bank0_full"), sem("max_bank1_full")]
        m_free = [sem("max_bank0_used"), sem("max_bank1_used")]
        e_full = [sem("exp_bank0_full"), sem("exp_bank1_full")]
        e_free = [sem("exp_bank0_used"), sem("exp_bank1_used")]
        s_qh, s_qm, s_qp = sem("q_high"), sem("q_middle"), sem("q_low")
        s_gather, s_kc = sem("q_rows_gathered"), sem("k_columns_ready")
        s_gd, s_ge, s_gated = sem("gate_differences"), sem("gate_exp"), sem("lora_middle_gated")
        s_nmp, s_nmrow = sem("max_parts_ready"), sem("max_rows_placed")
        s_masked, s_pv = sem("probs_masked"), sem("probs_slot0_used")
        s_xh = sem("xs_high_ready")
        s_sd, s_se, s_att1 = sem("scores1_ready"), sem("scores1_exp"), sem("attention1_done")
        s_sig, s_hh, s_hl = sem("gate_exp1"), sem("h_high_ready"), sem("h_low_ready")
        s_y, s_out = sem("y_ready"), sem("y_stored")
        s_held = sem("waits_held")
        d_w, d_a, d_b = sem("vector_setup_chain"), sem("vector_a_chain"), sem("vector_b_chain")

        def wait(eng, s, v):
            if not (isinstance(v, int) and v <= 0):
                eng.wait_ge(s, v)

        def hold(eng):
            eng.sem_inc(s_held, 1)

        def wait_full(eng, full, u, c, per):
            eng.wait_ge(full[u % 2], c * (per // 2) + (u // 2 + 1))

        def wait_free(eng, free, u, c, per):
            wait(eng, free[u % 2], c * (per // 2) + u // 2 + (free is b_free))

        def wait_used(eng, free, u, c, per):
            eng.wait_ge(free[u % 2], c * (per // 2) + (u // 2 + 1 + (free is b_free)))

        def run(eng, steps, chains=()):
            def do(names, ca, cb):
                for name in names:
                    if name[0] in steps:
                        steps[name[0]](ca if name[0][0] == "a" else cb, *name[1:])

            do(STAGE_A, 0, None)
            for ch in chains:
                ch.close()
            with eng.Fori(1, NCH) as c:
                do(interleave(STAGE_A, STAGE_B), c, c - 1)
                for ch in chains:
                    ch.close()
            do(STAGE_B, None, NCH - 1)

        class Chain:

            def __init__(self, eng, s, per):
                self.eng, self.s, self.per, self.n = eng, s, per, 0

            def link(self, c, ins):
                self.n += 1
                ins.then_inc(self.s, 1)
                self.eng.wait_ge(self.s, c * self.per + self.n)

            def close(self):
                assert self.n in (0, self.per), (self.n, self.per)
                self.n = 0

        x_v = x.rearrange("(c t p) h -> c p t h", p=P, t=NT)
        out_v = out.rearrange("(c t p) h -> c p t h", p=P, t=NT)
        qq_v = qq[:, :, :].rearrange("r (m j) t -> r j m t", m=NK)

        block = ctx.enter_context(nc.Block())

        constants = [(identf[:, :], ident_f), (identb[:, :], ident_b), (maskb[:, :], mask), (tri_sb[:, :, :], tri),
                     (kc[:, :, R_ALIBI:ROWS], k_cols), (qq[R_ALIBI:R_MAX, :, :], q_rows),
                     (qq[R_BLOCK:ROWS, :, :], q_blocks)]
        kp = "(k p) n -> p k n"
        weights = [(wq_sb[:, :, :], wqkv[:, 0:HID].rearrange(kp, p=P)),
                   (wtok[:, :, 0:C_L], wqkv[:, HID:HID + 2 * HD].rearrange(kp, p=P)),
                   (wtok[:, :, C_L:C_M], wr.rearrange(kp, p=P)),
                   (wtok[:, :, C_M:TOKC], lora_a.rearrange(kp, p=P)),
                   (wo_sb[:, 0:NK, :], wo.rearrange(kp, p=P)),
                   (wo_sb[P - NE * LR:P, NK, :], lora_b)]
        layer1_small = [(wq1_st, wq1.rearrange("(k p) d h -> p k d h", p=P)),
                        (bq_st, bq1.partition_broadcast(P)),
                        (bias48[:, HD:2 * HD], bk1.partition_broadcast(P)),
                        (bias48[:, 2 * HD:C1], bv1.partition_broadcast(P)),
                        (w48f[:, :, HD:2 * HD], wk1.rearrange(kp, p=P)),
                        (w48f[:, :, 2 * HD:C1], wv1.rearrange(kp, p=P)),
                        (sg[:, :], gate_s), (su[:, :], up_s), (dsb[:, :], down_s.partition_broadcast(P))]
        N_GATHER = len(PART_Q) * (P // HD)

        @block.sync
        def _(sp):
            def a_ln(c):
                if not isinstance(c, int):
                    for t in (NT - 2, NT - 1):
                        wait_used(sp, a_free, U_OUT + t, c - 1, UA)
                sp.dma_start(x_sb[:, :, :], x_v[c]).then_inc(s_x, 16)
                if isinstance(c, int):
                    for dst, src in constants:
                        sp.dma_start(dst, src).then_inc(s_const, 16)
                    for dst, src in weights:
                        sp.dma_start(dst, src).then_inc(s_w, 16)
                    for dst, src in layer1_small:
                        sp.dma_start(dst, src).then_inc(s_w1, 16)

            def a_q(c):
                sp.wait_ge(s_qp, c * NK + NK)
                for g, part in enumerate(PART_Q):
                    for j in range(P // HD):
                        sp.dma_start(qq_v[HD * g:HD * g + HD, j, :, :],
                                     qs[HD * j:HD * j + HD, part, :, :]).then_inc(s_gather, 16)

            def a_nm(c, b):
                wait_used(sp, a_free, U_NM0 if b == 0 else U_NM1, c, UA)
                for part in range(3):
                    sp.dma_start(qq[R_MAX + part:R_MAX + part + 1, :, b * SEQ:(b + 1) * SEQ],
                                 nmT[part * NH:(part + 1) * NH, b, :]).then_inc(s_nmrow, 16)

            def b_down(c, t):
                if t == NT - 1:
                    sp.wait_ge(s_y, c * NT + NT)
                    sp.dma_start(out_v[c], x1[:, :, :]).then_inc(s_out, 16)

            run(sp, {"a_ln": a_ln, "a_q": a_q, "a_nm": a_nm, "b_down": b_down})
            sp.wait_ge(s_out, 16 * NCH)

        @block.gpsimd
        def _(pool):
            pool.memset(mhalf[:, :], -0.5).then_inc(s_init, 1)
            pool.memset(vv[:, :, HD:HD + 1], 1.0).then_inc(s_init, 1)
            pool.memset(wo_sb[0:P - NE * LR, NK, :], 0.0).then_inc(s_init, 1)

            wd_flat = wd[:, :, :].rearrange("p i n -> p (i n)")
            pieces = ([(wgu[:, 0, k, :], gate_w[k * P:(k + 1) * P, :]) for k in range(NK)]
                      + [(wgu[:, 1, k, :], up_w[k * P:(k + 1) * P, :]) for k in range(NK)]
                      + [(wd_flat[:, q * INTER:(q + 1) * INTER], down_w[:, q * INTER:(q + 1) * INTER])
                         for q in range(NI * HID // INTER)])

            def load_piece(n):
                wait(pool, s_conv, n - NSTAGE + 1)
                pool.dma_start(stage[n % NSTAGE], pieces[n][1]).then_inc(s_stage[n % NSTAGE], 16)

            def convert(n):
                pool.wait_ge(s_stage[n % NSTAGE], 16 * (n // NSTAGE + 1))
                pool.tensor_copy(pieces[n][0], stage[n % NSTAGE]).then_inc(s_conv, 1)
                if n + NSTAGE < len(pieces):
                    load_piece(n + NSTAGE)

            def rstd(c, s_var, mv, rs, s_eps, s_rs):
                pool.wait_ge(s_var, c + 1)
                hold(pool)
                pool.tensor_scalar(rs[:, :], mv[:, :, 1], EPS, None, ALU.add).then_inc(s_eps, 1)
                pool.wait_ge(s_eps, c + 1)
                pool.tensor_tensor(rs[:, :], rs[:, :], mhalf[:, :], ALU.pow).then_inc(s_rs, 1)

            def a_ln(c):
                if isinstance(c, int):
                    for n in range(NSTAGE):
                        load_piece(n)
                    pool.wait_ge(s_init, 3)
                rstd(c, s_var0, mv0, rs0, s_eps0, s_rs0)
                if isinstance(c, int):
                    for n in range(3):
                        convert(n)

            def a_q(c):
                for m in range(NK):
                    wait_used(pool, a_free, U_Q + m, c, UA)
                    hold(pool)
                    pool.tensor_scalar(qs[:, 1, m, :], rq[:, m % 2, :], 1.0, None, ALU.mult).then_inc(s_qm, 1)
                    pool.wait_ge(s_qm, c * NK + m + 1)
                    pool.tensor_tensor(qs[:, 2, m, :], rq[:, m % 2, :], qs[:, 1, m, :], ALU.subtract)\
                        .then_inc(s_qp, 1)
                if isinstance(c, int):
                    for n in range(3, len(pieces)):
                        convert(n)
                    pool.wait_ge(s_cmax, 1)
                    pool.partition_all_reduce(cmax[:, 1:2], cmax[:, 0:1], P,
                                              bass.bass_isa.ReduceOp.max).then_inc(s_call, 1)

            def a_exp(c, b, g):
                n = b * NHG + g
                for u in (3 * n + 1, 3 * n + 2):
                    wait_used(pool, e_free, u, c, NB * SU)
                hold(pool)
                for w in (0, 2):
                    part = probs[:, n % 2, w, :].rearrange("p (h q) -> p h q", q=P)
                    pool.affine_select(out=part, in_=part, compare_op=ALU.is_ge, fill=0.0, base=0,
                                       pattern=[[0, HG], [1, P]], channel_multiplier=-1).then_inc(s_masked, 1)

            def b_ln(c):
                rstd(c, s_var1, mv1, rs1, s_eps1, s_rs1)

            def h_low(c, i):
                pool.wait_ge(s_hh, c * NI + i + 1)
                pool.tensor_tensor(hbuf[:, 1, i, :], hf[:, i % 2, :], hbuf[:, 0, i, :],
                                   ALU.subtract).then_inc(s_hl, 1)

            def b_gu(c, i):
                if i:
                    h_low(c, i - 1)

            def b_down(c, t):
                if t == 0:
                    h_low(c, NI - 1)

            run(pool, {"a_ln": a_ln, "a_q": a_q, "a_exp": a_exp, "b_ln": b_ln, "b_gu": b_gu, "b_down": b_down})

        @block.scalar
        def _(act):
            def a_xT(c):
                for k in range(NK):
                    u = U_XT + k
                    wait_full(act, a_full, u, c, UA)
                    act.activation(xT[:, k, :], ab[u % 2][:, :], ACT.Copy).then_inc(a_free[u % 2], 1)

            def a_q(c):
                for m in range(NK):
                    u = U_Q + m
                    wait_full(act, a_full, u, c, UA)
                    act.activation(qs[:, 0, m, :], ab[u % 2][:, :], ACT.Copy, scale=SCALE).then_inc(s_qh, 1)

            def a_kT(c):
                wait_full(act, a_full, U_KT, c, UA)
                act.activation(kk[:, :, :].rearrange("r t p -> r (t p)"),
                               ab[U_KT % 2][0:ROWS, 0:NT * P // 2].bitcast(BF16), ACT.Copy)\
                   .then_inc(a_free[U_KT % 2], 1)

            def a_gate(c):
                act.wait_ge(s_gd, c + 1)
                act.activation(gex[:, :, :], gex[:, :, :], ACT.Exp).then_inc(s_ge, 1)

            def a_nm(c, b):
                u = U_NM0 if b == 0 else U_NM1
                wait_full(act, a_full, u, c, UA)
                act.activation(nmT[:, b, :], ab[u % 2][0:3 * NH, 0:SEQ // 2].bitcast(BF16), ACT.Copy)\
                   .then_inc(a_free[u % 2], 1)

            def a_exp(c, b, g):
                n = b * NHG + g
                if n >= 2:
                    if n % 2 == 0:
                        act.wait_ge(s_pv, c * (NB * NHG // 2) + n // 2)
                    else:
                        wait_full(act, a_full, (U_PV0 if n - 2 < NHG else U_PV1) + (n - 2) % NHG // 2, c, UA)
                for w in range(3):
                    u = n * 3 + w
                    wait_full(act, e_full, u, c, NB * SU)
                    act.activation(probs[:, n % 2, w, :], eb[u % 2][:, :], ACT.Exp).then_inc(e_free[u % 2], 1)

            def a_attT(c):
                for k in range(NK + 1):
                    u = U_AT + k
                    wait_full(act, a_full, u, c, UA)
                    act.activation(attnT[:, k, :], ab[u % 2][:, :], ACT.Copy).then_inc(a_free[u % 2], 1)

            def b_xT(c):
                for k in range(NK):
                    u = V_XT + k
                    wait_full(act, b_full, u, c, UB)
                    act.activation(xs[:, 0, k, :], bb[u % 2][:, :], ACT.Copy, scale=XS).then_inc(s_xh, 1)

            def b_att(c):
                act.wait_ge(s_sd, c + 1)
                act.activation(S, S, ACT.Exp, scale=SCALE).then_inc(s_se, 1)

            def h_high(c, i):
                wait_used(act, b_free, V_GU + 2 * i + 1, c, UB)
                act.activation(hbuf[:, 0, i, :], hf[:, i % 2, :], ACT.Copy).then_inc(s_hh, 1)

            def b_gu(c, i):
                u = V_GU + 2 * i
                if i == 0:
                    act.wait_ge(s_wprep, 1)
                if i == 8:
                    act.wait_ge(s_att1, c + 1)
                wait_full(act, b_full, u, c, UB)
                if i >= 2:
                    wait_used(act, b_free, V_GU + 2 * (i - 2) + 1, c, UB)
                act.activation(ebuf[:, i % 2, :], bb[u % 2][:, :], ACT.Exp, scale=sg_neg[:, i:i + 1])\
                   .then_inc(s_sig, 1)
                if i:
                    h_high(c, i - 1)

            def b_down(c, t):
                if t == 0:
                    h_high(c, NI - 1)

            run(act, {"a_xT": a_xT, "a_q": a_q, "a_kT": a_kT, "a_gate": a_gate, "a_nm": a_nm, "a_exp": a_exp,
                      "a_attT": a_attT, "b_xT": b_xT, "b_att": b_att, "b_gu": b_gu, "b_down": b_down})

        @block.tensor
        def _(pe):
            def a_xT(c):
                if isinstance(c, int):
                    pe.wait_ge(s_const, 16 * len(constants))
                pe.wait_ge(s_xn0, c * NT + NT)
                for k in range(NK):
                    u = U_XT + k
                    wait_free(pe, a_free, u, c, UA)
                    for t in range(NT):
                        mm = pe.transpose(ab[u % 2][:, t * P:(t + 1) * P], xn0[:, t, k * P:(k + 1) * P],
                                          identf[:, :])
                    mm.then_inc(a_full[u % 2], 1)

            def a_tok(c):
                if isinstance(c, int):
                    pe.wait_ge(s_w, 16 * len(weights))
                for k in (NK - 2, NK - 1):
                    wait_used(pe, a_free, U_XT + k, c, UA)
                for w in range(2):
                    u = U_TOK + w
                    wait_free(pe, a_free, u, c, UA)
                    for t in (0, 1):
                        for k in range(NK):
                            mm = pe.matmul(ab[u % 2][:, t * TOKC:(t + 1) * TOKC],
                                           xT[:, k, (2 * w + t) * P:(2 * w + t + 1) * P], wtok[:, k, :],
                                           start=(k == 0), stop=(k == NK - 1))
                    mm.then_inc(a_full[u % 2], 1)

            def a_kT(c):
                pe.wait_ge(s_kc, c * 2 + 2)
                wait_free(pe, a_free, U_KT, c, UA)
                kb = ab[U_KT % 2][0:ROWS, 0:NT * P // 2].bitcast(BF16)
                for t in range(NT):
                    mm = pe.transpose(kb[:, t * P:(t + 1) * P], kc[:, t, :], identb[:, :])
                mm.then_inc(a_full[U_KT % 2], 1)

            def a_q(c):
                for m in range(NK):
                    u = U_Q + m
                    wait_free(pe, a_free, u, c, UA)
                    for k in range(NK):
                        mm = pe.matmul(ab[u % 2][:, :], wq_sb[:, k, m * P:(m + 1) * P], xT[:, k, :],
                                       start=(k == 0), stop=(k == NK - 1))
                    mm.then_inc(a_full[u % 2], 1)

            def a_max(c, b, g):
                n = b * NHG + g
                q0 = b * SEQ
                if n == 0:
                    pe.wait_ge(s_gather, 16 * N_GATHER * (c + 1))
                    wait_used(pe, a_free, U_KT, c, UA)
                for w in range(3):
                    u = 3 * n + w
                    bank = mb[u % 2]
                    wait_free(pe, m_free, u, c, NB * SU)
                    if w == 0:
                        pe.matmul(bank[:, :].rearrange("p (h k) -> p h k", h=HG), identb[:, :],
                                  maskb[:, :].unsqueeze(1).broadcast_to([P, HG, P]), start=True, stop=False,
                                  skip_group_check=True)
                        for j in range(HG):
                            mm = pe.matmul(bank[:, j * P:(j + 1) * P],
                                           qq[0:R_MAX, HG * g + j, q0:q0 + P], kk[0:R_MAX, 2 * b, :],
                                           start=False, stop=True, skip_group_check=True)
                    else:
                        pe.matmul(bank[:, :].rearrange("p (h k) -> p h k", h=2)[:, :, P:SEQ], identb[:, :],
                                  maskb[:, :].unsqueeze(1).broadcast_to([P, 2, P]), start=True, stop=False,
                                  skip_group_check=True)
                        for j in range(2):
                            mm = pe.matmul(bank[:, j * SEQ:(j + 1) * SEQ],
                                           qq[0:R_MAX, HG * g + 2 * (w - 1) + j, q0 + P:q0 + SEQ],
                                           kk[0:R_MAX, 2 * b:2 * b + 2, :].rearrange("r t p -> r (t p)"),
                                           start=False, stop=True, skip_group_check=True)
                    mm.then_inc(m_full[u % 2], 1)

            def a_nm(c, b):
                u = U_NM0 if b == 0 else U_NM1
                pe.wait_ge(s_nmp, c * NB + b + 1)
                wait_free(pe, a_free, u, c, UA)
                nb = ab[u % 2][0:3 * NH, 0:SEQ // 2].bitcast(BF16)
                for t in range(2):
                    mm = pe.transpose(nb[:, t * P:(t + 1) * P],
                                      nmp[:, b, t, :, :].rearrange("p a h -> p (a h)"), identb[:, :])
                mm.then_inc(a_full[u % 2], 1)

            def a_exp(c, b, g):
                n = b * NHG + g
                if g == 0:
                    pe.wait_ge(s_nmrow, 48 * (c * NB + b + 1))
                for w in range(3):
                    u = 3 * n + w
                    wait_free(pe, e_free, u, c, NB * SU)
                    kt, qt, rows = ((0, 0, ROWS), (0, 1, R_BLOCK), (1, 1, ROWS))[w]
                    pe.matmul(eb[u % 2][:, :], kk[0:rows, 2 * b + kt, :],
                              qq[0:rows, HG * g:HG * g + HG, b * SEQ + qt * P:b * SEQ + (qt + 1) * P],
                              start=True, stop=True)\
                      .then_inc(e_full[u % 2], 1)

            def a_pv(c, b, g):
                n = b * NHG + g
                u = (U_PV0 if b == 0 else U_PV1) + g // 2
                if g % 2 == 0:
                    wait_free(pe, a_free, u, c, UA)
                pe.wait_ge(s_masked, 2 * (c * NB * NHG + n + 1))
                pvb = ab[u % 2][:, 0:4 * HG * (HD + 1)].rearrange("p (t h d) -> p t h d", t=2, h=2 * HG)
                for j in range(HG):
                    p00, p01, p11 = (probs[:, n % 2, w, j * P:(j + 1) * P] for w in range(3))
                    h = (g % 2) * HG + j
                    pe.matmul(pvb[:, 0, h, :], p00, vv[:, 2 * b, :], start=True, stop=True)
                    pe.matmul(pvb[:, 1, h, :], p01, vv[:, 2 * b, :], start=True, stop=False)
                    mm = pe.matmul(pvb[:, 1, h, :], p11, vv[:, 2 * b + 1, :], start=False, stop=True)
                mm.then_inc(s_pv if g % 2 == 0 else a_full[u % 2], 1)

            def a_attT(c):
                pe.wait_ge(s_gated, c + 1)
                for u in (U_PV1 + 2, U_PV1 + 3):
                    wait_used(pe, a_free, u, c, UA)
                for k in range(NK + 1):
                    u = U_AT + k
                    wait_free(pe, a_free, u, c, UA)
                    for t in range(NT):
                        mm = pe.transpose(ab[u % 2][:, t * P:(t + 1) * P], attn[:, t, F0[k]:F0[k] + P],
                                          identf[:, :])
                    mm.then_inc(a_full[u % 2], 1)

            def a_out(c):
                for k in (NK - 1, NK):
                    wait_used(pe, a_free, U_AT + k, c, UA)
                for t in range(NT):
                    u = U_OUT + t
                    wait_free(pe, a_free, u, c, UA)
                    for k in range(NK + 1):
                        mm = pe.matmul(ab[u % 2][:, :], attnT[:, k, t * P:(t + 1) * P], wo_sb[:, k, :],
                                       start=(k == 0), stop=(k == NK))
                    mm.then_inc(a_full[u % 2], 1)

            def b_xT(c):
                pe.wait_ge(s_xn1, c * NT + NT)
                for k in range(NK):
                    u = V_XT + k
                    wait_free(pe, b_free, u, c, UB)
                    for t in range(NT):
                        mm = pe.transpose(bb[u % 2][:, t * P:(t + 1) * P], xn1[:, t, k * P:(k + 1) * P],
                                          identf[:, :])
                    mm.then_inc(b_full[u % 2], 1)

            def b_tok(c):
                for k in (NK - 2, NK - 1):
                    wait_used(pe, b_free, V_XT + k, c, UB)
                pe.wait_ge(s_wprep, 1)
                for w in range(2):
                    u = V_TOK + w
                    wait_free(pe, b_free, u, c, UB)
                    for t in (0, 1):
                        for k in range(NK):
                            for part in (0, 1):
                                mm = pe.matmul(bb[u % 2][:, t * 3 * C1:(t + 1) * 3 * C1],
                                               xs[:, part, k, (2 * w + t) * P:(2 * w + t + 1) * P],
                                               w48[:, k, :, :].rearrange("p a n -> p (a n)"),
                                               start=(k == 0 and part == 0), stop=(k == NK - 1 and part == 1))
                    mm.then_inc(b_full[u % 2], 1)

            def b_gu(c, i):
                if i == 0:
                    pe.wait_ge(s_conv, 3 * NK)
                for m in (0, 1):
                    u = V_GU + 2 * i + m
                    wait_free(pe, b_free, u, c, UB)
                    for k in range(NK):
                        for part in (0, 1):
                            mm = pe.matmul(bb[u % 2][:, :], wgu[:, m, k, i * P:(i + 1) * P], xs[:, part, k, :],
                                           start=(k == 0 and part == 0), stop=(k == NK - 1 and part == 1))
                    mm.then_inc(b_full[u % 2], 1)

            def b_down(c, t):
                u = V_DOWN + t
                wait_free(pe, b_free, u, c, UB)
                for i in range(NI):
                    if t == 0:
                        pe.wait_ge(s_hl, c * NI + i + 1)
                    for part in (0, 1):
                        mm = pe.matmul(bb[u % 2][:, :], hbuf[:, part, i, t * P:(t + 1) * P], wd[:, i, :],
                                       start=(i == 0 and part == 0), stop=(i == NI - 1 and part == 1))
                mm.then_inc(b_full[u % 2], 1)

            run(pe, {"a_xT": a_xT, "a_tok": a_tok, "a_kT": a_kT, "a_q": a_q, "a_max": a_max, "a_nm": a_nm,
                     "a_exp": a_exp, "a_pv": a_pv, "a_attT": a_attT, "a_out": a_out, "b_xT": b_xT, "b_tok": b_tok,
                     "b_gu": b_gu, "b_down": b_down})

        @block.vector
        def _(dve):
            ca = Chain(dve, d_a, 28)
            cb = Chain(dve, d_b, 38)
            for s in b_free:
                dve.sem_inc(s, 1)

            def layernorm(c, xin, st, mv, s_var, rs, s_rs, xn, s_xn, ch):
                for t in range(NT):
                    ins = dve.bn_stats(st[:, t, :], xin[:, t, :])
                ch.link(c, ins)
                hold(dve)
                for t in range(NT):
                    ins = dve.bn_aggr(mv[:, t, :], st[:, t, :])
                ins.then_inc(s_var, 1)
                dve.wait_ge(s_rs, c + 1)
                for t in range(NT):
                    dve.tensor_scalar(xn[:, t, :], xin[:, t, :], mv[:, t, 0:1], rs[:, t:t + 1],
                                      ALU.subtract, ALU.mult).then_inc(s_xn, 1)

            def a_ln(c):
                dve.wait_ge(s_x, 16 * (c + 1))
                layernorm(c, x_sb, st0, mv0, s_var0, rs0, s_rs0, xn0, s_xn0, ca)

            def a_tok(c):
                if isinstance(c, int):
                    dve.wait_ge(s_const, 16 * len(constants))
                for w in range(2):
                    u = U_TOK + w
                    ts = slice(2 * w, 2 * w + 2)
                    tok = ab[u % 2][:, 0:2 * TOKC].rearrange("p (t n) -> p t n", t=2)
                    wait_full(dve, a_full, u, c, UA)
                    dve.tensor_copy(lm[:, ts, :], tok[:, :, C_L:TOKC])
                    dve.tensor_copy(vv[:, ts, 0:HD], tok[:, :, C_V:C_L])
                    kg = kc[:, ts, 0:R_ALIBI].rearrange("p t (g d) -> p t g d", d=HD)
                    ca.link(c, dve.tensor_copy(kg[:, :, 0:5:2, :],
                                               tok[:, :, 0:HD].unsqueeze(2).broadcast_to([P, 2, 3, HD])))
                    dve.tensor_tensor(kres[:, ts, :], tok[:, :, 0:HD], kg[:, :, 0, :],
                                      ALU.subtract).then_inc(a_free[u % 2], 1)
                    wait_used(dve, a_free, u, c, UA)
                    ca.link(c, dve.tensor_copy(kg[:, :, 1:6:4, :],
                                               kres[:, ts, :].unsqueeze(2).broadcast_to([P, 2, 2, HD])))
                    dve.tensor_tensor(kg[:, :, 3, :], kres[:, ts, :], kg[:, :, 1, :],
                                      ALU.subtract).then_inc(s_kc, 1)

            def a_q(c):
                for m in range(NK):
                    u = U_Q + m
                    dve.wait_ge(s_qh, c * NK + m + 1)
                    if m >= 2:
                        dve.wait_ge(s_qp, c * NK + m - 1)
                    dve.scalar_tensor_tensor(out=rq[:, m % 2, :], in0=ab[u % 2][:, :], scalar=SCALE,
                                             in1=qs[:, 0, m, :], op0=ALU.mult,
                                             op1=ALU.subtract).then_inc(a_free[u % 2], 1)

            def a_gate(c):
                lg = lm[:, :, 0:NE]
                dve.wait_ge(s_kc, c * 2 + 2)
                ca.link(c, dve.tensor_reduce(gmx[:, :], lg, AX.X, ALU.max))
                dve.tensor_tensor(gex[:, :, :], lg, gmx[:, :].unsqueeze(2).broadcast_to([P, NT, NE]),
                                  ALU.subtract).then_inc(s_gd, 1)
                li = lg.unsqueeze(3).broadcast_to([P, NT, NE, NE])
                lj = lg.unsqueeze(2).broadcast_to([P, NT, NE, NE])
                dve.tensor_tensor(gcmp[:, :, :, :], lj, li, ALU.is_gt)
                ca.link(c, dve.tensor_tensor(geq[:, :, :, :], lj, li, ALU.is_equal))
                ca.link(c, dve.tensor_tensor(geq[:, :, :, :], geq[:, :, :, :],
                                             tri_sb[:, :, :].unsqueeze(1).broadcast_to([P, NT, NE, NE]), ALU.mult))
                ca.link(c, dve.tensor_tensor(gcmp[:, :, :, :], gcmp[:, :, :, :], geq[:, :, :, :], ALU.add))
                ca.link(c, dve.tensor_reduce(grk[:, :, :], gcmp[:, :, :, :], AX.X, ALU.add))
                dve.wait_ge(s_ge, c + 1)
                ca.link(c, dve.scalar_tensor_tensor(out=gate[:, :, :], in0=grk[:, :, :], scalar=2.0,
                                                    in1=gex[:, :, :], op0=ALU.is_lt, op1=ALU.mult))
                ca.link(c, dve.tensor_reduce(gsum[:, :], gate[:, :, :], AX.X, ALU.add))
                ca.link(c, dve.reciprocal(gsum[:, :], gsum[:, :]))
                ca.link(c, dve.scalar_tensor_tensor(out=gate[:, :, :], in0=gate[:, :, :], scalar=LORA_SCALE,
                                                    in1=gsum[:, :].unsqueeze(2).broadcast_to([P, NT, NE]),
                                                    op0=ALU.mult, op1=ALU.mult))
                dve.tensor_tensor(attn[:, :, HID:HID + NE * LR].rearrange("p t (e r) -> p t e r", e=NE),
                                  lm[:, :, NE:NE + NE * LR].rearrange("p t (e r) -> p t e r", e=NE),
                                  gate[:, :, :].unsqueeze(3).broadcast_to([P, NT, NE, LR]),
                                  ALU.mult).then_inc(s_gated, 1)
                if isinstance(c, int):
                    setup()

            def setup():
                n = [0]

                def link(ins):
                    n[0] += 1
                    ins.then_inc(d_w, 1)
                    dve.wait_ge(d_w, n[0])

                dve.wait_ge(s_w1, 16 * len(layer1_small))
                link(dve.tensor_tensor(sprod[:, :], sg[:, :], su[:, :], ALU.mult))
                link(dve.scalar_tensor_tensor(out=sprod[:, :], in0=sprod[:, :], scalar=-1.0, in1=sprod[:, :],
                                              op0=ALU.mult, op1=ALU.max))
                dve.tensor_reduce(cmax[:, 0:1], sprod[:, :], AX.X, ALU.max).then_inc(s_cmax, 1)
                link(dve.tensor_reduce(w48f[:, :, 0:HD], wq1_st, AX.X, ALU.add))
                link(dve.tensor_reduce(bias48[:, 0:HD], bq_st, AX.X, ALU.add))
                link(dve.tensor_copy(w48[:, :, 0, :], w48f[:, :, :]))
                link(dve.tensor_tensor(w48r[:, :, :], w48f[:, :, :], w48[:, :, 0, :], ALU.subtract))
                link(dve.tensor_copy(w48[:, :, 1, :], w48r[:, :, :]))
                link(dve.tensor_tensor(w48[:, :, 2, :], w48r[:, :, :], w48[:, :, 1, :], ALU.subtract))
                dve.tensor_scalar(sg_neg[:, :], sg[:, :], -1.0 / XS, None, ALU.mult)
                dve.tensor_scalar(sgx[:, :], sg[:, :], 1.0 / XS, None, ALU.mult)
                dve.wait_ge(s_call, 1)
                link(dve.tensor_scalar(cmax[:, 2:3], cmax[:, 1:2], 1e-30, None, ALU.max))
                link(dve.reciprocal(cmax[:, 3:4], cmax[:, 2:3]))
                dve.tensor_scalar(sux[:, :], su[:, :], cmax[:, 3:4], HS / XS, ALU.mult, ALU.mult)
                dve.tensor_scalar(dsb[:, :], dsb[:, :], cmax[:, 2:3], 1.0 / HS, ALU.mult,
                                  ALU.mult).then_inc(s_wprep, 1)

            def a_max(c, b, g):
                n = b * NHG + g
                for w in range(3):
                    u = 3 * n + w
                    wait_full(dve, m_full, u, c, NB * SU)
                    h0 = HG * g + (0 if w == 0 else 2 * (w - 1))
                    nh, nk = (HG, P) if w == 0 else (2, SEQ)
                    dve.tensor_reduce(mx[:, 2 * b + (w > 0), h0:h0 + nh],
                                      mb[u % 2][:, :].rearrange("p (h k) -> p h k", k=nk), AX.X,
                                      ALU.max).then_inc(m_free[u % 2], 1)

            def a_nm(c, b):
                for u in (SU * (b + 1) - 2, SU * (b + 1) - 1):
                    wait_used(dve, m_free, u, c, NB * SU)
                mv = mx[:, 2 * b:2 * b + 2, :]
                ca.link(c, dve.tensor_scalar(nmp[:, b, :, 0, :], mv, -1.0, None, ALU.mult))
                ca.link(c, dve.scalar_tensor_tensor(out=nres[:, :, :], in0=mv, scalar=-1.0, in1=nmp[:, b, :, 0, :],
                                                    op0=ALU.mult, op1=ALU.subtract))
                ca.link(c, dve.tensor_copy(nmp[:, b, :, 1, :], nres[:, :, :]))
                dve.tensor_tensor(nmp[:, b, :, 2, :], nres[:, :, :], nmp[:, b, :, 1, :],
                                  ALU.subtract).then_inc(s_nmp, 1)

            def a_pv(c, b, g):
                if g % 2 == 0:
                    return
                u = (U_PV0 if b == 0 else U_PV1) + g // 2
                wait_full(dve, a_full, u, c, UA)
                pvb = ab[u % 2][:, 0:4 * HG * (HD + 1)].rearrange("p (t h d) -> p t h d", t=2, h=2 * HG)
                if (b, g) != (0, 1):
                    wait_used(dve, a_free, u - 1 if g > 1 else U_PV0 + NHG // 2 - 1, c, UA)
                ca.link(c, dve.reciprocal(rden[:, :, :], pvb[:, :, :, HD]))
                h0 = 2 * HG * (g // 2)
                dve.tensor_tensor(attn[:, 2 * b:2 * b + 2, h0 * HD:(h0 + 2 * HG) * HD]
                                  .rearrange("p t (h d) -> p t h d", d=HD), pvb[:, :, :, 0:HD],
                                  rden[:, :, :].unsqueeze(3).broadcast_to([P, 2, 2 * HG, HD]),
                                  ALU.mult).then_inc(a_free[u % 2], 1)

            def a_out(c):
                wait(dve, s_out, 16 * c)
                for t in range(NT):
                    u = U_OUT + t
                    wait_full(dve, a_full, u, c, UA)
                    dve.tensor_tensor(x1[:, t, :], ab[u % 2][:, :], x_sb[:, t, :],
                                      ALU.add).then_inc(a_free[u % 2], 1)

            def b_ln(c):
                for t in (NT - 2, NT - 1):
                    wait_used(dve, a_free, U_OUT + t, c, UA)
                layernorm(c, x1, st1, mv1, s_var1, rs1, s_rs1, xn1, s_xn1, cb)

            def b_xT(c):
                for k in range(NK):
                    u = V_XT + k
                    dve.wait_ge(s_xh, c * NK + k + 1)
                    dve.scalar_tensor_tensor(out=xs[:, 1, k, :], in0=bb[u % 2][:, :], scalar=XS,
                                             in1=xs[:, 0, k, :], op0=ALU.mult,
                                             op1=ALU.subtract).then_inc(b_free[u % 2], 1)

            def b_tok(c):
                for w in range(2):
                    u = V_TOK + w
                    wait_full(dve, b_full, u, c, UB)
                    dve.tensor_reduce(t48[:, 2 * w:2 * w + 2, :],
                                      bb[u % 2][:, 0:6 * C1].rearrange("p (t a n) -> p t n a", t=2, a=3),
                                      AX.X, ALU.add).then_inc(b_free[u % 2], 1)
                for w in range(2):
                    wait_used(dve, b_free, V_TOK + w, c, UB)
                cb.link(c, dve.scalar_tensor_tensor(out=t48[:, :, :], in0=t48[:, :, :], scalar=1.0 / XS,
                                                    in1=bias48[:, :].unsqueeze(1).broadcast_to([P, NT, C1]),
                                                    op0=ALU.mult, op1=ALU.add))

            def b_att(c):
                q, k, v = t48[:, :, 0:HD], t48[:, :, HD:2 * HD], t48[:, :, 2 * HD:C1]
                full = [P, NT, HD, HD]
                dve.tensor_reduce(kext[:, 0, :], k, AX.X, ALU.max)
                cb.link(c, dve.tensor_reduce(kext[:, 1, :], k, AX.X, ALU.min))
                dve.tensor_tensor(m1[:, 0, :, :], q, kext[:, 0, :].unsqueeze(2).broadcast_to([P, NT, HD]), ALU.mult)
                cb.link(c, dve.tensor_tensor(m1[:, 1, :, :], q,
                                             kext[:, 1, :].unsqueeze(2).broadcast_to([P, NT, HD]), ALU.mult))
                dve.tensor_tensor(m1[:, 0, :, :], m1[:, 0, :, :], m1[:, 1, :, :], ALU.max)
                cb.link(c, dve.tensor_tensor(S, q.unsqueeze(3).broadcast_to(full), k.unsqueeze(2).broadcast_to(full),
                                             ALU.mult))
                dve.tensor_tensor(S, S, m1[:, 0, :, :].unsqueeze(3).broadcast_to(full), ALU.subtract)\
                   .then_inc(s_sd, 1)
                dve.wait_ge(s_se, c + 1)
                cb.link(c, dve.tensor_reduce(den1[:, :, :], S, AX.X, ALU.add))
                cb.link(c, dve.tensor_tensor(S, S, v.unsqueeze(2).broadcast_to(full), ALU.mult))
                dve.tensor_reduce(o1[:, :, :], S, AX.X, ALU.add).then_inc(s_att1, 1)
                cb.link(c, dve.reciprocal(den1[:, :, :], den1[:, :, :]))
                dve.wait_ge(s_att1, c + 1)
                cb.link(c, dve.tensor_tensor(o1[:, :, :], o1[:, :, :], den1[:, :, :], ALU.mult))
                x1v = x1[:, :, :].rearrange("p t (d h) -> p t d h", h=NH)
                cb.link(c, dve.tensor_tensor(x1v, x1v, o1[:, :, :].unsqueeze(3).broadcast_to([P, NT, HD, NH]),
                                             ALU.add))

            def b_gu(c, i):
                ug, uu = V_GU + 2 * i, V_GU + 2 * i + 1
                e = ebuf[:, i % 2, :]
                dve.wait_ge(s_sig, c * NI + i + 1)
                cb.link(c, dve.tensor_scalar(e, e, 1.0, None, ALU.add))
                cb.link(c, dve.reciprocal(e, e))
                if i >= 2:
                    dve.wait_ge(s_hl, c * NI + i - 1)
                dve.scalar_tensor_tensor(out=hf[:, i % 2, :], in0=bb[ug % 2][:, :], scalar=sgx[:, i:i + 1], in1=e,
                                         op0=ALU.mult, op1=ALU.mult).then_inc(b_free[ug % 2], 1)
                wait_used(dve, b_free, ug, c, UB)
                wait_full(dve, b_full, uu, c, UB)
                dve.scalar_tensor_tensor(out=hf[:, i % 2, :], in0=bb[uu % 2][:, :], scalar=sux[:, i:i + 1],
                                         in1=hf[:, i % 2, :], op0=ALU.mult, op1=ALU.mult).then_inc(b_free[uu % 2], 1)

            def b_down(c, t):
                u = V_DOWN + t
                wait_full(dve, b_full, u, c, UB)
                if t:
                    dve.wait_ge(s_y, c * NT + t)
                dve.tensor_tensor(ytmp[:, :], bb[u % 2][:, :], dsb[:, :], ALU.mult).then_inc(b_free[u % 2], 1)
                wait_used(dve, b_free, u, c, UB)
                dve.tensor_tensor(x1[:, t, :], x1[:, t, :], ytmp[:, :], ALU.add).then_inc(s_y, 1)

            run(dve, {"a_ln": a_ln, "a_tok": a_tok, "a_q": a_q, "a_gate": a_gate, "a_max": a_max, "a_nm": a_nm,
                      "a_pv": a_pv, "a_out": a_out, "b_ln": b_ln, "b_xT": b_xT, "b_tok": b_tok, "b_att": b_att,
                      "b_gu": b_gu, "b_down": b_down}, (ca, cb))


def _parts(a, n=3):
    out, rest = [], np.asarray(a, np.float64)
    for _ in range(n):
        p = rest.astype(np.dtype("bfloat16"))
        out.append(p)
        rest = rest - p.astype(np.float64)
    return np.stack(out)


def _constants():
    bf = np.dtype("bfloat16")
    base = 2.0 ** (-2.0 ** (-(math.log2(NH) - 3)))
    slopes = (base ** np.arange(1, NH + 1, dtype=np.float64)).astype(np.float32).astype(np.float64)
    pos = np.arange(SEQ, dtype=np.float64)
    q_rows = np.zeros((6, NH, CHUNK), bf)
    q_rows[0:3] = _parts(slopes)[:, :, None]
    q_rows[3:6] = np.tile(_parts(-slopes[:, None] * pos[None, :]), (1, 1, NB))
    blk = np.arange(P) // MB
    q_blocks = np.where(blk[None, :] < np.arange(1, P // MB)[:, None], -1e30, 0.0).astype(bf)
    k_cols = np.ones((P, NT, ROWS - R_ALIBI), bf)
    k_cols[:, :, R_BLOCK - R_ALIBI:] = (blk[:, None] == np.arange(1, P // MB)[None, :])[:, None, :]
    for t in range(NT):
        k_cols[:, t, 0:3] = ((t % (SEQ // P)) * P + np.arange(P))[:, None]
    i = np.arange(P)
    return {
        "q_rows": q_rows,
        "q_blocks": np.tile(q_blocks[:, None, :], (1, NH, CHUNK // P)),
        "k_cols": k_cols,
        "mask": np.where(i[None, :] > i[:, None], -1e30, 0.0).astype(bf),
        "ident_f": np.eye(P, dtype=np.float32), "ident_b": np.eye(P, dtype=bf),
        "tri": np.tile(np.tril(np.ones((NE, NE), np.float32), -1)[None], (P, 1, 1)),
    }


def kernel(**inputs):
    import concourse.bacc as _bacc
    from concourse.bass_utils import run_bass_kernel_spmd as _run

    a = {k: np.asarray(v) for k, v in inputs.items()}
    laid = {
        "x": a["L0_attn_hidden_states"].reshape(BATCH * SEQ, HID),
        "wqkv": a["L0_attn_Wqkv"], "wo": a["L0_attn_Wo"],
        "lora_a": a["L0_ffn_A"].reshape(NE * LR, HID).T,
        "lora_b": a["L0_ffn_B"].transpose(0, 2, 1).reshape(NE * LR, HID),
        "wr": a["L0_ffn_Wr"].T,
        "wq1": a["L1_attn_Wq"], "bq1": a["L1_attn_bq"],
        "wk1": a["L1_attn_Wk"].reshape(HID, HD), "bk1": a["L1_attn_bk"].reshape(HD),
        "wv1": a["L1_attn_Wv"].reshape(HID, HD), "bv1": a["L1_attn_bv"].reshape(HD),
        "gate_w": a["L1_ffn_gate_wq"].T, "gate_s": a["L1_ffn_gate_scale"].reshape(NI, P).T,
        "up_w": a["L1_ffn_up_wq"].T, "up_s": a["L1_ffn_up_scale"].reshape(NI, P).T,
        "down_w": a["L1_ffn_down_wq"].T.reshape(NI, P, HID).transpose(1, 0, 2).reshape(P, NI * HID),
        "down_s": a["L1_ffn_down_scale"],
    }
    laid.update(_constants())

    nc = _bacc.Bacc("TRN2", target_bir_lowering=False, num_devices=1)
    arrays, args = {}, []
    for name, v in laid.items():
        v = np.ascontiguousarray(v)
        arrays[f"in_{name}"] = v
        args.append(nc.dram_tensor(f"in_{name}", v.shape, mybir.dt.from_np(v.dtype), kind="ExternalInput").ap())
    args.append(nc.dram_tensor("out_y", (BATCH * SEQ, HID), F32, kind="ExternalOutput").ap())
    build(nc, *args)
    r = _run(nc, [arrays], core_ids=[0])
    return r.results[0]["out_y"].reshape(BATCH, SEQ, HID)
```

```python
import math
from contextlib import ExitStack

import numpy as np
import concourse.bass as bass
from concourse import mybir

P = 128
BATCH, SEQ, HID = 8, 256, 512
NH, HD = 32, 16
CHUNK = 512
NCH = BATCH * SEQ // CHUNK
NT = CHUNK // P
NK = HID // P
NB = CHUNK // SEQ
HG = 4
NHG = NH // HG
NE, LR = 4, 16
INTER = 1792
NI = INTER // P
EPS = 1e-5
SCALE = HD ** -0.5
LORA_SCALE = 16.0 / math.sqrt(16.0)

PART_Q = [0, 0, 1, 0, 2, 1]
PART_K = [0, 1, 0, 2, 0, 1]
R_ALIBI = 6 * HD
R_MAX = R_ALIBI + 6
R_BLOCK = R_MAX + 3
MB = 8
ROWS = R_BLOCK + P // MB - 1

TOKC = 2 * HD + NE + NE * LR
C_V, C_L, C_M = HD, 2 * HD, 2 * HD + NE
C1 = 3 * HD
XS = 256.0
HS = 2.0 ** -17

U_XT, U_TOK, U_Q, U_KT, U_NM, U_PV, U_AT, U_OUT = 0, 4, 6, 10, (11, 15), ((12, 13, 14, 16), (17, 18, 19, 20)), 21, 26
UA = 30
F0 = [k * P for k in range(NK)] + [HID + NE * LR - P]
V_XT, V_TOK, V_GU, V_DOWN = 0, 4, 6, 6 + 2 * NI
UB = V_DOWN + NT
NSTAGE = 4
SU = 3 * NHG

F32, BF16, F16, I32 = mybir.dt.float32, mybir.dt.bfloat16, mybir.dt.float16, mybir.dt.int32
ALU = mybir.AluOpType
ACT = mybir.ActivationFunctionType
AX = mybir.AxisListType

HEAD = [("a_ln", t) for t in range(NT + 1)] + [("a_xT",), ("a_tok",), ("a_q",), ("a_kT",), ("a_gate",)]
TAIL = [("a_attT",), ("a_out", 0), ("a_out", 1), ("a_ln1", 0), ("a_out", 2), ("a_ln1", 1), ("a_out", 3),
        ("a_ln1", 2), ("a_ln1", 3), ("a_ln1", 4)]


def attention(fill):
    out = []
    for g in range(NHG):
        out += [("a_max", 0, g)] + fill()
    out += [("a_nm", 0), ("a_max", 1, 0)] + fill() + [("a_max", 1, 1)] + fill()
    for g in range(NHG):
        out += [("a_max", 1, g + 2)] if g + 2 < NHG else []
        out += [("a_nm", 1)] if g + 2 == NHG else []
        out += [("a_exp", 0, g)] + ([("a_pv", 0, g - 1)] if g else []) + fill()
    out += [("a_exp", 1, 0), ("a_pv", 0, NHG - 1)]
    for g in range(1, NHG):
        out += [("a_exp", 1, g), ("a_pv", 1, g - 1)] + fill()
    return out + [("a_pv", 1, NHG - 1)]


def pipelined():
    gu = [("b_gu", i) for i in range(NI)]
    down = [("b_down", t) for t in range(NT)]
    head = [("b_xT",), ("a_ln", 0), ("a_ln", 1), ("b_tok",), ("a_ln", 2), ("a_ln", 3), ("a_ln", 4), gu[0],
            ("a_xT",), gu[1], ("a_tok",), ("a_q",), gu[2], ("a_kT",), ("b_att",), gu[3], ("a_gate",), ("b_att2",),
            gu[4], gu[5], gu[6]]
    rest = gu[7:] + down
    slots = iter(PLACES)

    def fill():
        return [rest.pop(0) for _ in range(next(slots))]

    body = attention(fill)
    assert not rest
    return head + body + TAIL


PLACES = [0, 0, 1, 0, 0, 1, 0, 0] + [1, 0] + [0, 1, 0, 1, 0, 1, 0, 1] + [0, 1, 1, 1, 1, 0, 0]
STAGE_A = HEAD + attention(lambda: []) + TAIL
STAGE_B = ([("b_xT",), ("b_tok",), ("b_gu", 0), ("b_att",), ("b_gu", 1), ("b_att2",)]
           + [("b_gu", i) for i in range(2, NI)] + [("b_down", t) for t in range(NT)])


def build(nc, x, wqkv, wo, lora_a, lora_b, wr, wq1, bq1, wk1, bk1, wv1, bv1,
          gate_w, gate_s, up_w, up_s, down_w, down_s, q_rows, q_blocks, k_cols, mask, ident_f, ident_b, tri, out):
    with ExitStack() as ctx:
        def sb(name, shape, dt):
            return ctx.enter_context(nc.sbuf_tensor(name, shape, dt))

        def sem(name):
            return ctx.enter_context(nc.semaphore(name))

        identf = sb("identf", [P, P], F32)
        identb = sb("identb", [P, P], BF16)
        maskb = sb("maskb", [P, P], BF16)
        tri_sb = sb("tri_sb", [P, NE, NE], F32)
        wq_sb = sb("wq_sb", [P, NK, HID], F32)
        wtok = sb("wtok", [P, NK, TOKC], F32)
        wo_sb = sb("wo_sb", [P, NK + 1, HID], F32)
        w48f = sb("w48f", [P, NK, C1], F32)
        w48r = sb("w48r", [P, NK, C1], F32)
        w48 = sb("w48", [P, NK, 3, C1], BF16)
        bias48 = sb("bias48", [P, C1], F32)
        wgu = sb("wgu", [P, 2, NK, INTER], F16)
        wd = sb("wd", [P, NI, HID], F16)
        sg = sb("sg", [P, NI], F32)
        su = sb("su", [P, NI], F32)
        sgx = sb("sgx", [P, NI], F32)
        sux = sb("sux", [P, NI], F32)
        sprod = sb("sprod", [P, NI], F32)
        cmax = sb("cmax", [P, 4], F32)
        dsb = sb("dsb", [P, HID], F32)
        x_sb = sb("x_sb", [P, NT, HID], F32)
        attn = sb("attn", [P, NT, HID + NE * LR], F32)
        xn0 = attn[:, :, 0:HID]
        st0 = sb("st0", [P, NT, 6], F32)
        mv0 = sb("mv0", [P, NT, 2], F32)
        rs0 = sb("rs0", [P, NT], F32)
        mhalf = sb("mhalf", [P, NT], F32)
        qparts = sb("qparts", [P, 3 * NK * CHUNK], BF16)
        qs = qparts[:, :].rearrange("p (a m t) -> p a m t", a=3, m=NK)
        attnT = qparts[:, 0:5 * CHUNK * 2].bitcast(F32).rearrange("p (k t) -> p k t", k=5)
        rq = sb("rq", [P, 2, CHUNK], F32)
        probs = sb("probs", [P, 2, 3, CHUNK], F32)
        xT = probs[:, :, :, :].rearrange("p s u t -> p (s u) t")[:, 0:NK, :]
        kc = sb("kc", [P, NT, ROWS], BF16)
        kres = sb("kres", [P, NT, HD], F32)
        kk = sb("kk", [ROWS, NT, P], BF16)
        vv = sb("vv", [P, NT, HD + 1], F32)
        qq = sb("qq", [ROWS, NH, CHUNK], BF16)
        mx = sb("mx", [P, NT, NH], F32)
        nres = sb("nres", [P, 2, NH], F32)
        nmp = sb("nmp", [P, NB, 2, 3, NH], BF16)
        nmT = sb("nmT", [3 * NH, NB, SEQ], BF16)
        rden = sb("rden", [P, 2, 2 * HG], F32)
        lm = sb("lm", [P, NT, NE + NE * LR], F32)
        gate = sb("gate", [P, NT, NE], F32)
        gsum = sb("gsum", [P, NT], F32)
        gmx = sb("gmx", [P, NT], F32)
        gex = sb("gex", [P, NT, NE], F32)
        gcmp = sb("gcmp", [P, NT, NE, NE], F32)
        geq = sb("geq", [P, NT, NE, NE], F32)
        grk = sb("grk", [P, NT, NE], F32)
        x1 = sb("x1", [P, NT, HID], F32)
        st1 = sb("st1", [P, NT, 6], F32)
        mv1 = sb("mv1", [P, NT, 2], F32)
        rs1 = sb("rs1", [P, NT], F32)
        hbuf = sb("hbuf", [P, 2, NI, CHUNK], F16)
        hflat = hbuf[:, :, :, :].rearrange("p a i t -> p (a i t)")
        xn1 = hflat[:, 0:NT * HID * 2].bitcast(F32).rearrange("p (t h) -> p t h", t=NT)
        S = hflat[:, NT * HID * 2:NT * (HID + HD * HD) * 2].bitcast(F32).rearrange(
            "p (t d e) -> p t d e", t=NT, d=HD)
        stage = [hflat[:, s * INTER * 2:(s + 1) * INTER * 2].bitcast(I32) for s in range(NSTAGE)]
        xs = sb("xs", [P, 2, NK, CHUNK], F16)
        wq1_st = xs[:, :, :, :].rearrange("p a k t -> p (a k t)").bitcast(F32).rearrange(
            "p (k d h) -> p k d h", k=NK, h=NH)
        t48 = sb("t48", [P, NT, C1], F32)
        kext = sb("kext", [P, 2, NT], F32)
        m1 = sb("m1", [P, 2, NT, HD], F32)
        den1 = sb("den1", [P, NT, HD], F32)
        o1 = sb("o1", [P, NT, HD], F32)
        ebuf = sb("ebuf", [P, 2, CHUNK], F32)
        hf = sb("hf", [P, 2, CHUNK], F32)
        ytmp = sb("ytmp", [P, HID], F32)
        bq_st = ytmp[:, :].rearrange("p (d h) -> p d h", h=NH)

        def bank(name, dt=F32, n=512):
            return ctx.enter_context(nc.psum_tensor(name, [P, n], dt))

        ab = [bank("a_bank0"), bank("a_bank1")]
        bb = [bank("b_bank0"), bank("b_bank1")]
        mb = [bank("max_bank0"), bank("max_bank1")]
        eb = [bank("exp_bank0"), bank("exp_bank1")]

        s_const, s_w, s_w1 = sem("constants_loaded"), sem("weights_loaded"), sem("layer1_small_loaded")
        s_init = sem("pool_constants_set")
        s_stage = [sem(f"stage{i}_loaded") for i in range(NSTAGE)]
        s_conv = sem("ffn_weights_converted")
        s_cmax, s_call, s_wprep = sem("scale_product_ready"), sem("scale_maximum_ready"), sem("layer1_operands_ready")
        s_x = [sem(f"x_tile{t}_loaded") for t in range(NT)]
        s_var0, s_eps0, s_rs0, s_xn0 = sem("variance0"), sem("variance0_plus_eps"), sem("rstd0"), sem("xn0_ready")
        s_var1, s_eps1, s_rs1, s_xn1 = sem("variance1"), sem("variance1_plus_eps"), sem("rstd1"), sem("xn1_ready")
        a_full = [sem("a_bank0_full"), sem("a_bank1_full")]
        a_free = [sem("a_bank0_used"), sem("a_bank1_used")]
        b_full = [sem("b_bank0_full"), sem("b_bank1_full")]
        b_free = [sem("b_bank0_used"), sem("b_bank1_used")]
        m_full = [sem("max_bank0_full"), sem("max_bank1_full")]
        m_free = [sem("max_bank0_used"), sem("max_bank1_used")]
        e_full = [sem("exp_bank0_full"), sem("exp_bank1_full")]
        e_free = [sem("exp_bank0_used"), sem("exp_bank1_used")]
        s_qh, s_qm, s_qp = sem("q_high"), sem("q_middle"), sem("q_low")
        s_qd = [sem(f"q_tile{m}_in_dram") for m in range(NK)]
        s_gather, s_kc = sem("q_rows_gathered"), sem("k_columns_ready")
        s_gd, s_ge, s_gated = sem("gate_differences"), sem("gate_exp"), sem("lora_middle_gated")
        s_nmp, s_nmrow = sem("max_parts_ready"), sem("max_rows_placed")
        s_masked, s_pv = sem("probs_masked"), sem("probs_slot0_used")
        s_xh = sem("xs_high_ready")
        s_sd, s_se, s_att1 = sem("scores1_ready"), sem("scores1_exp"), sem("attention1_done")
        s_sig, s_hh, s_hl = sem("gate_exp1"), sem("h_high_ready"), sem("h_low_ready")
        s_y = sem("y_ready")
        s_out = [sem(f"y_tile{t}_stored") for t in range(NT)]
        s_held = sem("waits_held")
        d_w, d_a, d_b = sem("vector_setup_chain"), sem("vector_a_chain"), sem("vector_b_chain")

        def wait(eng, s, v):
            if not (isinstance(v, int) and v <= 0):
                eng.wait_ge(s, v)

        def hold(eng):
            eng.sem_inc(s_held, 1)

        def wait_full(eng, full, u, c, per):
            eng.wait_ge(full[u % 2], c * (per // 2) + (u // 2 + 1))

        def wait_free(eng, free, u, c, per):
            wait(eng, free[u % 2], c * (per // 2) + u // 2 + (free is b_free))

        def wait_used(eng, free, u, c, per):
            eng.wait_ge(free[u % 2], c * (per // 2) + (u // 2 + 1 + (free is b_free)))

        def run(eng, steps, chains=()):
            def do(names, ca, cb):
                for name in names:
                    if name[0] in steps:
                        steps[name[0]](ca if name[0][0] == "a" else cb, *name[1:])

            do(STAGE_A, 0, None)
            for ch in chains:
                ch.close()
            with eng.Fori(1, NCH) as c:
                do(pipelined(), c, c - 1)
                for ch in chains:
                    ch.close()
            do(STAGE_B, None, NCH - 1)

        class Chain:

            def __init__(self, eng, s, per):
                self.eng, self.s, self.per, self.n = eng, s, per, 0

            def link(self, c, ins):
                self.n += 1
                ins.then_inc(self.s, 1)
                self.eng.wait_ge(self.s, c * self.per + self.n)

            def close(self):
                assert self.n in (0, self.per), (self.n, self.per)
                self.n = 0

        x_v = x.rearrange("(c t p) h -> c p t h", p=P, t=NT)
        out_v = out.rearrange("(c t p) h -> c p t h", p=P, t=NT)
        q_dram = nc.dram_tensor("q_parts", [3, NH * HD, CHUNK], BF16).ap()

        block = ctx.enter_context(nc.Block())

        constants = [(identf[:, :], ident_f), (identb[:, :], ident_b), (maskb[:, :], mask), (tri_sb[:, :, :], tri),
                     (kc[:, :, R_ALIBI:ROWS], k_cols), (qq[R_ALIBI:R_MAX, :, :], q_rows),
                     (qq[R_BLOCK:ROWS, :, :], q_blocks)]
        kp = "(k p) n -> p k n"
        weights = [(wq_sb[:, :, :], wqkv[:, 0:HID].rearrange(kp, p=P)),
                   (wtok[:, :, 0:C_L], wqkv[:, HID:HID + 2 * HD].rearrange(kp, p=P)),
                   (wtok[:, :, C_L:C_M], wr.rearrange(kp, p=P)),
                   (wtok[:, :, C_M:TOKC], lora_a.rearrange(kp, p=P)),
                   (wo_sb[:, 0:NK, :], wo.rearrange(kp, p=P)),
                   (wo_sb[P - NE * LR:P, NK, :], lora_b)]
        layer1_small = [(wq1_st, wq1.rearrange("(k p) d h -> p k d h", p=P)),
                        (bq_st, bq1.partition_broadcast(P)),
                        (bias48[:, HD:2 * HD], bk1.partition_broadcast(P)),
                        (bias48[:, 2 * HD:C1], bv1.partition_broadcast(P)),
                        (w48f[:, :, HD:2 * HD], wk1.rearrange(kp, p=P)),
                        (w48f[:, :, 2 * HD:C1], wv1.rearrange(kp, p=P)),
                        (sg[:, :], gate_s), (su[:, :], up_s), (dsb[:, :], down_s.partition_broadcast(P))]
        wd_flat = wd[:, :, :].rearrange("p i n -> p (i n)")
        pieces = ([(wgu[:, 0, k, :], gate_w[k * P:(k + 1) * P, :]) for k in range(NK)]
                  + [(wgu[:, 1, k, :], up_w[k * P:(k + 1) * P, :]) for k in range(NK)]
                  + [(wd_flat[:, q * INTER:(q + 1) * INTER], down_w[:, q * INTER:(q + 1) * INTER])
                     for q in range(NI * HID // INTER)])
        N_GATHER = len(PART_Q) * 2

        @block.sync
        def _(sp):
            def a_ln(c, t):
                if t < NT:
                    if not isinstance(c, int):
                        wait_used(sp, a_free, U_OUT + t, c - 1, UA)
                    sp.dma_start(x_sb[:, t, :], x_v[c][:, t, :]).then_inc(s_x[t], 16)
                if isinstance(c, int) and t == NT:
                    for dst, src in constants:
                        sp.dma_start(dst, src).then_inc(s_const, 16)
                    for dst, src in weights:
                        sp.dma_start(dst, src).then_inc(s_w, 16)
                    for dst, src in layer1_small:
                        sp.dma_start(dst, src).then_inc(s_w1, 16)

            def a_q(c):
                for m in range(NK):
                    sp.wait_ge(s_qp, c * NK + m + 1)
                    sp.dma_start(q_dram[:, m * P:(m + 1) * P, :].rearrange("a r t -> r a t"),
                                 qs[:, :, m, :]).then_inc(s_qd[m], 16)
                for half in range(2):
                    for m in (2 * half, 2 * half + 1):
                        sp.wait_ge(s_qd[m], 16 * (c + 1))
                    hs = slice(half * NH // 2, (half + 1) * NH // 2)
                    for g, part in enumerate(PART_Q):
                        sp.dma_start(qq[HD * g:HD * g + HD, hs, :],
                                     q_dram[part].rearrange("(h d) t -> d h t", d=HD)[:, hs, :])\
                          .then_inc(s_gather, 16)

            def a_nm(c, b):
                wait_used(sp, a_free, U_NM[b], c, UA)
                for part in range(3):
                    sp.dma_start(qq[R_MAX + part:R_MAX + part + 1, :, b * SEQ:(b + 1) * SEQ],
                                 nmT[part * NH:(part + 1) * NH, b, :]).then_inc(s_nmrow, 16)

            def b_down(c, t):
                sp.wait_ge(s_y, c * NT + t + 1)
                sp.dma_start(out_v[c][:, t, :], x1[:, t, :]).then_inc(s_out[t], 16)

            run(sp, {"a_ln": a_ln, "a_q": a_q, "a_nm": a_nm, "b_down": b_down})
            for t in range(NT):
                sp.wait_ge(s_out[t], 16 * NCH)

        @block.gpsimd
        def _(pool):
            pool.memset(mhalf[:, :], -0.5).then_inc(s_init, 1)
            pool.memset(vv[:, :, HD:HD + 1], 1.0).then_inc(s_init, 1)
            pool.memset(wo_sb[0:P - NE * LR, NK, :], 0.0).then_inc(s_init, 1)

            def load_piece(n):
                wait(pool, s_conv, n - NSTAGE + 1)
                pool.dma_start(stage[n % NSTAGE], pieces[n][1]).then_inc(s_stage[n % NSTAGE], 16)

            def rstd(c, t, s_var, mv, rs, s_eps, s_rs):
                pool.wait_ge(s_var, c * NT + t + 1)
                hold(pool)
                pool.tensor_scalar(rs[:, t:t + 1], mv[:, t, 1:2], EPS, None, ALU.add).then_inc(s_eps, 1)
                pool.wait_ge(s_eps, c * NT + t + 1)
                pool.tensor_tensor(rs[:, t:t + 1], rs[:, t:t + 1], mhalf[:, t:t + 1], ALU.pow).then_inc(s_rs, 1)

            def a_ln(c, t):
                if isinstance(c, int) and t == 0:
                    for n in range(NSTAGE):
                        load_piece(n)
                    pool.wait_ge(s_init, 3)
                if t < NT:
                    rstd(c, t, s_var0, mv0, rs0, s_eps0, s_rs0)

            def a_max(c, b, g):
                n = b * NHG + g + NSTAGE
                if isinstance(c, int) and n < len(pieces):
                    load_piece(n)

            def a_nm(c, b):
                if isinstance(c, int) and b == 0:
                    pool.wait_ge(s_cmax, 1)
                    pool.partition_all_reduce(cmax[:, 1:2], cmax[:, 0:1], P,
                                              bass.bass_isa.ReduceOp.max).then_inc(s_call, 1)

            def a_q(c):
                for m in range(NK):
                    wait_used(pool, a_free, U_Q + m, c, UA)
                    hold(pool)
                    pool.tensor_scalar(qs[:, 1, m, :], rq[:, m % 2, :], 1.0, None, ALU.mult).then_inc(s_qm, 1)
                    pool.wait_ge(s_qm, c * NK + m + 1)
                    pool.tensor_tensor(qs[:, 2, m, :], rq[:, m % 2, :], qs[:, 1, m, :], ALU.subtract)\
                        .then_inc(s_qp, 1)

            def a_exp(c, b, g):
                n = b * NHG + g
                for u in (3 * n + 1, 3 * n + 2):
                    wait_used(pool, e_free, u, c, NB * SU)
                hold(pool)
                for w in (0, 2):
                    part = probs[:, n % 2, w, :].rearrange("p (h q) -> p h q", q=P)
                    pool.affine_select(out=part, in_=part, compare_op=ALU.is_ge, fill=0.0, base=0,
                                       pattern=[[0, HG], [1, P]], channel_multiplier=-1).then_inc(s_masked, 1)

            def a_ln1(c, t):
                if t < NT:
                    rstd(c, t, s_var1, mv1, rs1, s_eps1, s_rs1)

            def h_low(c, i):
                pool.wait_ge(s_hh, c * NI + i + 1)
                pool.tensor_tensor(hbuf[:, 1, i, :], hf[:, i % 2, :], hbuf[:, 0, i, :],
                                   ALU.subtract).then_inc(s_hl, 1)

            def b_gu(c, i):
                if i:
                    h_low(c, i - 1)

            def b_down(c, t):
                if t == 0:
                    h_low(c, NI - 1)

            run(pool, {"a_ln": a_ln, "a_q": a_q, "a_max": a_max, "a_nm": a_nm, "a_exp": a_exp, "a_ln1": a_ln1, "b_gu": b_gu, "b_down": b_down})

        @block.scalar
        def _(act):
            def a_xT(c):
                for k in range(NK):
                    u = U_XT + k
                    wait_full(act, a_full, u, c, UA)
                    act.activation(xT[:, k, :], ab[u % 2][:, :], ACT.Copy).then_inc(a_free[u % 2], 1)

            def a_q(c):
                for m in range(NK):
                    u = U_Q + m
                    wait_full(act, a_full, u, c, UA)
                    act.activation(qs[:, 0, m, :], ab[u % 2][:, :], ACT.Copy, scale=SCALE).then_inc(s_qh, 1)

            def a_kT(c):
                wait_full(act, a_full, U_KT, c, UA)
                act.activation(kk[:, :, :].rearrange("r t p -> r (t p)"),
                               ab[U_KT % 2][0:ROWS, 0:NT * P // 2].bitcast(BF16), ACT.Copy)\
                   .then_inc(a_free[U_KT % 2], 1)

            def a_max(c, b, g):
                n = b * NHG + g
                if isinstance(c, int) and n < len(pieces):
                    act.wait_ge(s_stage[n % NSTAGE], 16 * (n // NSTAGE + 1))
                    act.activation(pieces[n][0], stage[n % NSTAGE], ACT.Copy).then_inc(s_conv, 1)

            def a_gate(c):
                act.wait_ge(s_gd, c + 1)
                act.activation(gex[:, :, :], gex[:, :, :], ACT.Exp).then_inc(s_ge, 1)

            def a_nm(c, b):
                u = U_NM[b]
                wait_full(act, a_full, u, c, UA)
                act.activation(nmT[:, b, :], ab[u % 2][0:3 * NH, 0:SEQ // 2].bitcast(BF16), ACT.Copy)\
                   .then_inc(a_free[u % 2], 1)

            def a_exp(c, b, g):
                n = b * NHG + g
                if n >= 2:
                    if n % 2 == 0:
                        act.wait_ge(s_pv, c * (NB * NHG // 2) + n // 2)
                    else:
                        wait_full(act, a_full, U_PV[(n - 2) // NHG][(n - 2) % NHG // 2], c, UA)
                for w in range(3):
                    u = n * 3 + w
                    wait_full(act, e_full, u, c, NB * SU)
                    act.activation(probs[:, n % 2, w, :], eb[u % 2][:, :], ACT.Exp).then_inc(e_free[u % 2], 1)

            def a_attT(c):
                for k in range(NK + 1):
                    u = U_AT + k
                    wait_full(act, a_full, u, c, UA)
                    act.activation(attnT[:, k, :], ab[u % 2][:, :], ACT.Copy).then_inc(a_free[u % 2], 1)

            def b_xT(c):
                for k in range(NK):
                    u = V_XT + k
                    wait_full(act, b_full, u, c, UB)
                    act.activation(xs[:, 0, k, :], bb[u % 2][:, :], ACT.Copy, scale=XS).then_inc(s_xh, 1)

            def b_att(c):
                act.wait_ge(s_sd, c + 1)
                act.activation(S, S, ACT.Exp, scale=SCALE).then_inc(s_se, 1)

            def h_high(c, i):
                wait_used(act, b_free, V_GU + 2 * i + 1, c, UB)
                act.activation(hbuf[:, 0, i, :], hf[:, i % 2, :], ACT.Copy).then_inc(s_hh, 1)

            def b_gu(c, i):
                u = V_GU + 2 * i
                if i == 0:
                    act.wait_ge(s_wprep, 1)
                if i == 8:
                    act.wait_ge(s_att1, c + 1)
                wait_full(act, b_full, u, c, UB)
                if i >= 2:
                    wait_used(act, b_free, V_GU + 2 * (i - 2) + 1, c, UB)
                act.activation(ebuf[:, i % 2, :], bb[u % 2][:, :], ACT.Tanh, scale=sgx[:, i:i + 1])\
                   .then_inc(s_sig, 1)
                if i:
                    h_high(c, i - 1)

            def b_down(c, t):
                if t == 0:
                    h_high(c, NI - 1)

            run(act, {"a_xT": a_xT, "a_q": a_q, "a_kT": a_kT, "a_gate": a_gate, "a_max": a_max, "a_nm": a_nm,
                      "a_exp": a_exp, "a_attT": a_attT, "b_xT": b_xT, "b_att": b_att, "b_gu": b_gu, "b_down": b_down})

        @block.tensor
        def _(pe):
            def a_xT(c):
                if isinstance(c, int):
                    pe.wait_ge(s_const, 16 * len(constants))
                pe.wait_ge(s_xn0, c * NT + NT)
                for k in range(NK):
                    u = U_XT + k
                    wait_free(pe, a_free, u, c, UA)
                    for t in range(NT):
                        mm = pe.transpose(ab[u % 2][:, t * P:(t + 1) * P], xn0[:, t, k * P:(k + 1) * P],
                                          identf[:, :])
                    mm.then_inc(a_full[u % 2], 1)

            def a_tok(c):
                if isinstance(c, int):
                    pe.wait_ge(s_w, 16 * len(weights))
                for k in (NK - 2, NK - 1):
                    wait_used(pe, a_free, U_XT + k, c, UA)
                for w in range(2):
                    u = U_TOK + w
                    wait_free(pe, a_free, u, c, UA)
                    for t in (0, 1):
                        for k in range(NK):
                            mm = pe.matmul(ab[u % 2][:, t * TOKC:(t + 1) * TOKC],
                                           xT[:, k, (2 * w + t) * P:(2 * w + t + 1) * P], wtok[:, k, :],
                                           start=(k == 0), stop=(k == NK - 1))
                    mm.then_inc(a_full[u % 2], 1)

            def a_kT(c):
                pe.wait_ge(s_kc, c * 2 + 2)
                wait_free(pe, a_free, U_KT, c, UA)
                kb = ab[U_KT % 2][0:ROWS, 0:NT * P // 2].bitcast(BF16)
                for t in range(NT):
                    mm = pe.transpose(kb[:, t * P:(t + 1) * P], kc[:, t, :], identb[:, :])
                mm.then_inc(a_full[U_KT % 2], 1)

            def a_q(c):
                for m in range(NK):
                    u = U_Q + m
                    wait_free(pe, a_free, u, c, UA)
                    for k in range(NK):
                        mm = pe.matmul(ab[u % 2][:, :], wq_sb[:, k, m * P:(m + 1) * P], xT[:, k, :],
                                       start=(k == 0), stop=(k == NK - 1))
                    mm.then_inc(a_full[u % 2], 1)

            def a_max(c, b, g):
                n = b * NHG + g
                q0 = b * SEQ
                if n == 0:
                    pe.wait_ge(s_gather, 16 * N_GATHER * (c + 1))
                    wait_used(pe, a_free, U_KT, c, UA)
                for w in range(3):
                    u = 3 * n + w
                    bank = mb[u % 2]
                    wait_free(pe, m_free, u, c, NB * SU)
                    if w == 0:
                        pe.matmul(bank[:, :].rearrange("p (h k) -> p h k", h=HG), identb[:, :],
                                  maskb[:, :].unsqueeze(1).broadcast_to([P, HG, P]), start=True, stop=False,
                                  skip_group_check=True)
                        for j in range(HG):
                            mm = pe.matmul(bank[:, j * P:(j + 1) * P],
                                           qq[0:R_MAX, HG * g + j, q0:q0 + P], kk[0:R_MAX, 2 * b, :],
                                           start=False, stop=True, skip_group_check=True)
                    else:
                        pe.matmul(bank[:, :].rearrange("p (h k) -> p h k", h=2)[:, :, P:SEQ], identb[:, :],
                                  maskb[:, :].unsqueeze(1).broadcast_to([P, 2, P]), start=True, stop=False,
                                  skip_group_check=True)
                        for j in range(2):
                            mm = pe.matmul(bank[:, j * SEQ:(j + 1) * SEQ],
                                           qq[0:R_MAX, HG * g + 2 * (w - 1) + j, q0 + P:q0 + SEQ],
                                           kk[0:R_MAX, 2 * b:2 * b + 2, :].rearrange("r t p -> r (t p)"),
                                           start=False, stop=True, skip_group_check=True)
                    mm.then_inc(m_full[u % 2], 1)

            def a_nm(c, b):
                u = U_NM[b]
                pe.wait_ge(s_nmp, c * NB + b + 1)
                wait_free(pe, a_free, u, c, UA)
                nb = ab[u % 2][0:3 * NH, 0:SEQ // 2].bitcast(BF16)
                for t in range(2):
                    mm = pe.transpose(nb[:, t * P:(t + 1) * P],
                                      nmp[:, b, t, :, :].rearrange("p a h -> p (a h)"), identb[:, :])
                mm.then_inc(a_full[u % 2], 1)

            def a_exp(c, b, g):
                n = b * NHG + g
                if g == 0:
                    pe.wait_ge(s_nmrow, 48 * (c * NB + b + 1))
                for w in range(3):
                    u = 3 * n + w
                    wait_free(pe, e_free, u, c, NB * SU)
                    kt, qt, rows = ((0, 0, ROWS), (0, 1, R_BLOCK), (1, 1, ROWS))[w]
                    pe.matmul(eb[u % 2][:, :], kk[0:rows, 2 * b + kt, :],
                              qq[0:rows, HG * g:HG * g + HG, b * SEQ + qt * P:b * SEQ + (qt + 1) * P],
                              start=True, stop=True)\
                      .then_inc(e_full[u % 2], 1)

            def a_pv(c, b, g):
                n = b * NHG + g
                u = U_PV[b][g // 2]
                if g % 2 == 0:
                    wait_free(pe, a_free, u, c, UA)
                pe.wait_ge(s_masked, 2 * (c * NB * NHG + n + 1))
                pvb = ab[u % 2][:, 0:4 * HG * (HD + 1)].rearrange("p (t h d) -> p t h d", t=2, h=2 * HG)
                for j in range(HG):
                    p00, p01, p11 = (probs[:, n % 2, w, j * P:(j + 1) * P] for w in range(3))
                    h = (g % 2) * HG + j
                    pe.matmul(pvb[:, 0, h, :], p00, vv[:, 2 * b, :], start=True, stop=True)
                    pe.matmul(pvb[:, 1, h, :], p01, vv[:, 2 * b, :], start=True, stop=False)
                    mm = pe.matmul(pvb[:, 1, h, :], p11, vv[:, 2 * b + 1, :], start=False, stop=True)
                mm.then_inc(s_pv if g % 2 == 0 else a_full[u % 2], 1)

            def a_attT(c):
                pe.wait_ge(s_gated, c + 1)
                for u in U_PV[1][-2:]:
                    wait_used(pe, a_free, u, c, UA)
                for k in range(NK + 1):
                    u = U_AT + k
                    wait_free(pe, a_free, u, c, UA)
                    for t in range(NT):
                        mm = pe.transpose(ab[u % 2][:, t * P:(t + 1) * P], attn[:, t, F0[k]:F0[k] + P],
                                          identf[:, :])
                    mm.then_inc(a_full[u % 2], 1)

            def a_out(c, t):
                if t == 0:
                    for k in (NK - 1, NK):
                        wait_used(pe, a_free, U_AT + k, c, UA)
                u = U_OUT + t
                wait_free(pe, a_free, u, c, UA)
                for k in range(NK + 1):
                    mm = pe.matmul(ab[u % 2][:, :], attnT[:, k, t * P:(t + 1) * P], wo_sb[:, k, :],
                                   start=(k == 0), stop=(k == NK))
                mm.then_inc(a_full[u % 2], 1)

            def b_xT(c):
                pe.wait_ge(s_xn1, c * NT + NT)
                for k in range(NK):
                    u = V_XT + k
                    wait_free(pe, b_free, u, c, UB)
                    for t in range(NT):
                        mm = pe.transpose(bb[u % 2][:, t * P:(t + 1) * P], xn1[:, t, k * P:(k + 1) * P],
                                          identf[:, :])
                    mm.then_inc(b_full[u % 2], 1)

            def b_tok(c):
                for k in (NK - 2, NK - 1):
                    wait_used(pe, b_free, V_XT + k, c, UB)
                pe.wait_ge(s_wprep, 1)
                for w in range(2):
                    u = V_TOK + w
                    wait_free(pe, b_free, u, c, UB)
                    for t in (0, 1):
                        for k in range(NK):
                            for part in (0, 1):
                                mm = pe.matmul(bb[u % 2][:, t * 3 * C1:(t + 1) * 3 * C1],
                                               xs[:, part, k, (2 * w + t) * P:(2 * w + t + 1) * P],
                                               w48[:, k, :, :].rearrange("p a n -> p (a n)"),
                                               start=(k == 0 and part == 0), stop=(k == NK - 1 and part == 1))
                    mm.then_inc(b_full[u % 2], 1)

            def b_gu(c, i):
                if i == 0:
                    pe.wait_ge(s_conv, 3 * NK)
                for m in (0, 1):
                    u = V_GU + 2 * i + m
                    wait_free(pe, b_free, u, c, UB)
                    for k in range(NK):
                        for part in (0, 1):
                            mm = pe.matmul(bb[u % 2][:, :], wgu[:, m, k, i * P:(i + 1) * P], xs[:, part, k, :],
                                           start=(k == 0 and part == 0), stop=(k == NK - 1 and part == 1))
                    mm.then_inc(b_full[u % 2], 1)

            def b_down(c, t):
                u = V_DOWN + t
                wait_free(pe, b_free, u, c, UB)
                for i in range(NI):
                    if t == 0:
                        pe.wait_ge(s_hl, c * NI + i + 1)
                    for part in (0, 1):
                        mm = pe.matmul(bb[u % 2][:, :], hbuf[:, part, i, t * P:(t + 1) * P], wd[:, i, :],
                                       start=(i == 0 and part == 0), stop=(i == NI - 1 and part == 1))
                mm.then_inc(b_full[u % 2], 1)

            run(pe, {"a_xT": a_xT, "a_tok": a_tok, "a_kT": a_kT, "a_q": a_q, "a_max": a_max, "a_nm": a_nm,
                     "a_exp": a_exp, "a_pv": a_pv, "a_attT": a_attT, "a_out": a_out, "b_xT": b_xT, "b_tok": b_tok,
                     "b_gu": b_gu, "b_down": b_down})

        @block.vector
        def _(dve):
            ca = Chain(dve, d_a, 35)
            cb = Chain(dve, d_b, 9)
            for s in b_free:
                dve.sem_inc(s, 1)

            def layernorm(c, t, xin, st, mv, s_var, rs, s_rs, xn, s_xn, ch):
                if t < NT:
                    ch.link(c, dve.bn_stats(st[:, t, :], xin[:, t, :]))
                    hold(dve)
                    dve.bn_aggr(mv[:, t, :], st[:, t, :]).then_inc(s_var, 1)
                if t:
                    dve.wait_ge(s_rs, c * NT + t)
                    dve.tensor_scalar(xn[:, t - 1, :], xin[:, t - 1, :], mv[:, t - 1, 0:1], rs[:, t - 1:t],
                                      ALU.subtract, ALU.mult).then_inc(s_xn, 1)

            def a_ln(c, t):
                if t < NT:
                    dve.wait_ge(s_x[t], 16 * (c + 1))
                layernorm(c, t, x_sb, st0, mv0, s_var0, rs0, s_rs0, xn0, s_xn0, ca)

            def a_ln1(c, t):
                if t < NT:
                    wait_used(dve, a_free, U_OUT + t, c, UA)
                layernorm(c, t, x1, st1, mv1, s_var1, rs1, s_rs1, xn1, s_xn1, ca)

            def a_tok(c):
                if isinstance(c, int):
                    dve.wait_ge(s_const, 16 * len(constants))
                for w in range(2):
                    u = U_TOK + w
                    ts = slice(2 * w, 2 * w + 2)
                    tok = ab[u % 2][:, 0:2 * TOKC].rearrange("p (t n) -> p t n", t=2)
                    wait_full(dve, a_full, u, c, UA)
                    dve.tensor_copy(lm[:, ts, :], tok[:, :, C_L:TOKC])
                    dve.tensor_copy(vv[:, ts, 0:HD], tok[:, :, C_V:C_L])
                    kg = kc[:, ts, 0:R_ALIBI].rearrange("p t (g d) -> p t g d", d=HD)
                    ca.link(c, dve.tensor_copy(kg[:, :, 0:5:2, :],
                                               tok[:, :, 0:HD].unsqueeze(2).broadcast_to([P, 2, 3, HD])))
                    dve.tensor_tensor(kres[:, ts, :], tok[:, :, 0:HD], kg[:, :, 0, :],
                                      ALU.subtract).then_inc(a_free[u % 2], 1)
                    wait_used(dve, a_free, u, c, UA)
                    ca.link(c, dve.tensor_copy(kg[:, :, 1:6:4, :],
                                               kres[:, ts, :].unsqueeze(2).broadcast_to([P, 2, 2, HD])))
                    dve.tensor_tensor(kg[:, :, 3, :], kres[:, ts, :], kg[:, :, 1, :],
                                      ALU.subtract).then_inc(s_kc, 1)

            def a_q(c):
                for m in range(NK):
                    u = U_Q + m
                    dve.wait_ge(s_qh, c * NK + m + 1)
                    if m >= 2:
                        dve.wait_ge(s_qp, c * NK + m - 1)
                    dve.scalar_tensor_tensor(out=rq[:, m % 2, :], in0=ab[u % 2][:, :], scalar=SCALE,
                                             in1=qs[:, 0, m, :], op0=ALU.mult,
                                             op1=ALU.subtract).then_inc(a_free[u % 2], 1)

            def a_gate(c):
                lg = lm[:, :, 0:NE]
                dve.wait_ge(s_kc, c * 2 + 2)
                ca.link(c, dve.tensor_reduce(gmx[:, :], lg, AX.X, ALU.max))
                dve.tensor_tensor(gex[:, :, :], lg, gmx[:, :].unsqueeze(2).broadcast_to([P, NT, NE]),
                                  ALU.subtract).then_inc(s_gd, 1)
                li = lg.unsqueeze(3).broadcast_to([P, NT, NE, NE])
                lj = lg.unsqueeze(2).broadcast_to([P, NT, NE, NE])
                dve.tensor_tensor(gcmp[:, :, :, :], lj, li, ALU.is_gt)
                ca.link(c, dve.tensor_tensor(geq[:, :, :, :], lj, li, ALU.is_equal))
                ca.link(c, dve.tensor_tensor(geq[:, :, :, :], geq[:, :, :, :],
                                             tri_sb[:, :, :].unsqueeze(1).broadcast_to([P, NT, NE, NE]), ALU.mult))
                ca.link(c, dve.tensor_tensor(gcmp[:, :, :, :], gcmp[:, :, :, :], geq[:, :, :, :], ALU.add))
                ca.link(c, dve.tensor_reduce(grk[:, :, :], gcmp[:, :, :, :], AX.X, ALU.add))
                dve.wait_ge(s_ge, c + 1)
                ca.link(c, dve.scalar_tensor_tensor(out=gate[:, :, :], in0=grk[:, :, :], scalar=2.0,
                                                    in1=gex[:, :, :], op0=ALU.is_lt, op1=ALU.mult))
                ca.link(c, dve.tensor_reduce(gsum[:, :], gate[:, :, :], AX.X, ALU.add))
                ca.link(c, dve.reciprocal(gsum[:, :], gsum[:, :]))
                ca.link(c, dve.scalar_tensor_tensor(out=gate[:, :, :], in0=gate[:, :, :], scalar=LORA_SCALE,
                                                    in1=gsum[:, :].unsqueeze(2).broadcast_to([P, NT, NE]),
                                                    op0=ALU.mult, op1=ALU.mult))
                dve.tensor_tensor(attn[:, :, HID:HID + NE * LR].rearrange("p t (e r) -> p t e r", e=NE),
                                  lm[:, :, NE:NE + NE * LR].rearrange("p t (e r) -> p t e r", e=NE),
                                  gate[:, :, :].unsqueeze(3).broadcast_to([P, NT, NE, LR]),
                                  ALU.mult).then_inc(s_gated, 1)
                if isinstance(c, int):
                    setup()

            def setup():
                n = [0]

                def link(ins):
                    n[0] += 1
                    ins.then_inc(d_w, 1)
                    dve.wait_ge(d_w, n[0])

                dve.wait_ge(s_w1, 16 * len(layer1_small))
                link(dve.tensor_tensor(sprod[:, :], sg[:, :], su[:, :], ALU.mult))
                link(dve.scalar_tensor_tensor(out=sprod[:, :], in0=sprod[:, :], scalar=-1.0, in1=sprod[:, :],
                                              op0=ALU.mult, op1=ALU.max))
                dve.tensor_reduce(cmax[:, 0:1], sprod[:, :], AX.X, ALU.max).then_inc(s_cmax, 1)
                link(dve.tensor_reduce(w48f[:, :, 0:HD], wq1_st, AX.X, ALU.add))
                link(dve.tensor_reduce(bias48[:, 0:HD], bq_st, AX.X, ALU.add))
                link(dve.tensor_copy(w48[:, :, 0, :], w48f[:, :, :]))
                link(dve.tensor_tensor(w48r[:, :, :], w48f[:, :, :], w48[:, :, 0, :], ALU.subtract))
                link(dve.tensor_copy(w48[:, :, 1, :], w48r[:, :, :]))
                link(dve.tensor_tensor(w48[:, :, 2, :], w48r[:, :, :], w48[:, :, 1, :], ALU.subtract))
                dve.tensor_scalar(sgx[:, :], sg[:, :], 0.5 / XS, None, ALU.mult)
                dve.wait_ge(s_call, 1)
                link(dve.tensor_scalar(cmax[:, 2:3], cmax[:, 1:2], 1e-30, None, ALU.max))
                link(dve.reciprocal(cmax[:, 3:4], cmax[:, 2:3]))
                link(dve.tensor_scalar(sux[:, :], su[:, :], cmax[:, 3:4], HS / XS, ALU.mult, ALU.mult))
                link(dve.tensor_tensor(sux[:, :], sux[:, :], sgx[:, :], ALU.mult))
                dve.tensor_scalar(dsb[:, :], dsb[:, :], cmax[:, 2:3], 1.0 / HS, ALU.mult,
                                  ALU.mult).then_inc(s_wprep, 1)

            def a_max(c, b, g):
                n = b * NHG + g
                for w in range(3):
                    u = 3 * n + w
                    wait_full(dve, m_full, u, c, NB * SU)
                    h0 = HG * g + (0 if w == 0 else 2 * (w - 1))
                    nh, nk = (HG, P) if w == 0 else (2, SEQ)
                    dve.tensor_reduce(mx[:, 2 * b + (w > 0), h0:h0 + nh],
                                      mb[u % 2][:, :].rearrange("p (h k) -> p h k", k=nk), AX.X,
                                      ALU.max).then_inc(m_free[u % 2], 1)

            def a_nm(c, b):
                for u in (SU * (b + 1) - 2, SU * (b + 1) - 1):
                    wait_used(dve, m_free, u, c, NB * SU)
                mv = mx[:, 2 * b:2 * b + 2, :]
                ca.link(c, dve.tensor_scalar(nmp[:, b, :, 0, :], mv, -1.0, None, ALU.mult))
                ca.link(c, dve.scalar_tensor_tensor(out=nres[:, :, :], in0=mv, scalar=-1.0, in1=nmp[:, b, :, 0, :],
                                                    op0=ALU.mult, op1=ALU.subtract))
                ca.link(c, dve.tensor_copy(nmp[:, b, :, 1, :], nres[:, :, :]))
                dve.tensor_tensor(nmp[:, b, :, 2, :], nres[:, :, :], nmp[:, b, :, 1, :],
                                  ALU.subtract).then_inc(s_nmp, 1)

            def a_pv(c, b, g):
                if g % 2 == 0:
                    return
                u = U_PV[b][g // 2]
                wait_full(dve, a_full, u, c, UA)
                pvb = ab[u % 2][:, 0:4 * HG * (HD + 1)].rearrange("p (t h d) -> p t h d", t=2, h=2 * HG)
                if (b, g) != (0, 1):
                    wait_used(dve, a_free, U_PV[b][g // 2 - 1] if g > 1 else U_PV[0][-1], c, UA)
                ca.link(c, dve.reciprocal(rden[:, :, :], pvb[:, :, :, HD]))
                h0 = 2 * HG * (g // 2)
                dve.tensor_tensor(attn[:, 2 * b:2 * b + 2, h0 * HD:(h0 + 2 * HG) * HD]
                                  .rearrange("p t (h d) -> p t h d", d=HD), pvb[:, :, :, 0:HD],
                                  rden[:, :, :].unsqueeze(3).broadcast_to([P, 2, 2 * HG, HD]),
                                  ALU.mult).then_inc(a_free[u % 2], 1)

            def a_out(c, t):
                wait(dve, s_out[t], 16 * c)
                u = U_OUT + t
                wait_full(dve, a_full, u, c, UA)
                dve.tensor_tensor(x1[:, t, :], ab[u % 2][:, :], x_sb[:, t, :],
                                  ALU.add).then_inc(a_free[u % 2], 1)

            def b_xT(c):
                for k in range(NK):
                    u = V_XT + k
                    dve.wait_ge(s_xh, c * NK + k + 1)
                    dve.scalar_tensor_tensor(out=xs[:, 1, k, :], in0=bb[u % 2][:, :], scalar=XS,
                                             in1=xs[:, 0, k, :], op0=ALU.mult,
                                             op1=ALU.subtract).then_inc(b_free[u % 2], 1)

            def b_tok(c):
                for w in range(2):
                    u = V_TOK + w
                    wait_full(dve, b_full, u, c, UB)
                    dve.tensor_reduce(t48[:, 2 * w:2 * w + 2, :],
                                      bb[u % 2][:, 0:6 * C1].rearrange("p (t a n) -> p t n a", t=2, a=3),
                                      AX.X, ALU.add).then_inc(b_free[u % 2], 1)
                for w in range(2):
                    wait_used(dve, b_free, V_TOK + w, c, UB)
                cb.link(c, dve.scalar_tensor_tensor(out=t48[:, :, :], in0=t48[:, :, :], scalar=1.0 / XS,
                                                    in1=bias48[:, :].unsqueeze(1).broadcast_to([P, NT, C1]),
                                                    op0=ALU.mult, op1=ALU.add))

            def b_att(c):
                q, k = t48[:, :, 0:HD], t48[:, :, HD:2 * HD]
                full = [P, NT, HD, HD]
                dve.tensor_reduce(kext[:, 0, :], k, AX.X, ALU.max)
                cb.link(c, dve.tensor_reduce(kext[:, 1, :], k, AX.X, ALU.min))
                dve.tensor_tensor(m1[:, 0, :, :], q, kext[:, 0, :].unsqueeze(2).broadcast_to([P, NT, HD]), ALU.mult)
                cb.link(c, dve.tensor_tensor(m1[:, 1, :, :], q,
                                             kext[:, 1, :].unsqueeze(2).broadcast_to([P, NT, HD]), ALU.mult))
                dve.tensor_tensor(m1[:, 0, :, :], m1[:, 0, :, :], m1[:, 1, :, :], ALU.max)
                cb.link(c, dve.tensor_tensor(S, q.unsqueeze(3).broadcast_to(full), k.unsqueeze(2).broadcast_to(full),
                                             ALU.mult))
                dve.tensor_tensor(S, S, m1[:, 0, :, :].unsqueeze(3).broadcast_to(full), ALU.subtract)\
                   .then_inc(s_sd, 1)

            def b_att2(c):
                v = t48[:, :, 2 * HD:C1]
                full = [P, NT, HD, HD]
                dve.wait_ge(s_se, c + 1)
                cb.link(c, dve.tensor_reduce(den1[:, :, :], S, AX.X, ALU.add))
                cb.link(c, dve.tensor_tensor(S, S, v.unsqueeze(2).broadcast_to(full), ALU.mult))
                dve.tensor_reduce(o1[:, :, :], S, AX.X, ALU.add).then_inc(s_att1, 1)
                cb.link(c, dve.reciprocal(den1[:, :, :], den1[:, :, :]))
                dve.wait_ge(s_att1, c + 1)
                cb.link(c, dve.tensor_tensor(o1[:, :, :], o1[:, :, :], den1[:, :, :], ALU.mult))
                x1v = x1[:, :, :].rearrange("p t (d h) -> p t d h", h=NH)
                cb.link(c, dve.tensor_tensor(x1v, x1v, o1[:, :, :].unsqueeze(3).broadcast_to([P, NT, HD, NH]),
                                             ALU.add))

            def b_gu(c, i):
                ug, uu = V_GU + 2 * i, V_GU + 2 * i + 1
                dve.wait_ge(s_sig, c * NI + i + 1)
                if i >= 2:
                    dve.wait_ge(s_hl, c * NI + i - 1)
                dve.scalar_tensor_tensor(out=hf[:, i % 2, :], in0=ebuf[:, i % 2, :], scalar=1.0,
                                         in1=bb[ug % 2][:, :], op0=ALU.add,
                                         op1=ALU.mult).then_inc(b_free[ug % 2], 1)
                wait_used(dve, b_free, ug, c, UB)
                wait_full(dve, b_full, uu, c, UB)
                dve.scalar_tensor_tensor(out=hf[:, i % 2, :], in0=bb[uu % 2][:, :], scalar=sux[:, i:i + 1],
                                         in1=hf[:, i % 2, :], op0=ALU.mult, op1=ALU.mult)\
                   .then_inc(b_free[uu % 2], 1)

            def b_down(c, t):
                u = V_DOWN + t
                wait_full(dve, b_full, u, c, UB)
                if t:
                    dve.wait_ge(s_y, c * NT + t)
                dve.tensor_tensor(ytmp[:, :], bb[u % 2][:, :], dsb[:, :], ALU.mult).then_inc(b_free[u % 2], 1)
                wait_used(dve, b_free, u, c, UB)
                dve.tensor_tensor(x1[:, t, :], x1[:, t, :], ytmp[:, :], ALU.add).then_inc(s_y, 1)

            run(dve, {"a_ln": a_ln, "a_tok": a_tok, "a_q": a_q, "a_gate": a_gate, "a_max": a_max, "a_nm": a_nm,
                      "a_pv": a_pv, "a_out": a_out, "a_ln1": a_ln1, "b_xT": b_xT, "b_tok": b_tok, "b_att": b_att,
                      "b_att2": b_att2,
                      "b_gu": b_gu, "b_down": b_down}, (ca, cb))


def _parts(a, n=3):
    out, rest = [], np.asarray(a, np.float64)
    for _ in range(n):
        p = rest.astype(np.dtype("bfloat16"))
        out.append(p)
        rest = rest - p.astype(np.float64)
    return np.stack(out)


def _constants():
    bf = np.dtype("bfloat16")
    base = 2.0 ** (-2.0 ** (-(math.log2(NH) - 3)))
    slopes = (base ** np.arange(1, NH + 1, dtype=np.float64)).astype(np.float32).astype(np.float64)
    pos = np.arange(SEQ, dtype=np.float64)
    q_rows = np.zeros((6, NH, CHUNK), bf)
    q_rows[0:3] = _parts(slopes)[:, :, None]
    q_rows[3:6] = np.tile(_parts(-slopes[:, None] * pos[None, :]), (1, 1, NB))
    blk = np.arange(P) // MB
    q_blocks = np.where(blk[None, :] < np.arange(1, P // MB)[:, None], -1e30, 0.0).astype(bf)
    k_cols = np.ones((P, NT, ROWS - R_ALIBI), bf)
    k_cols[:, :, R_BLOCK - R_ALIBI:] = (blk[:, None] == np.arange(1, P // MB)[None, :])[:, None, :]
    for t in range(NT):
        k_cols[:, t, 0:3] = ((t % (SEQ // P)) * P + np.arange(P))[:, None]
    i = np.arange(P)
    return {
        "q_rows": q_rows,
        "q_blocks": np.tile(q_blocks[:, None, :], (1, NH, CHUNK // P)),
        "k_cols": k_cols,
        "mask": np.where(i[None, :] > i[:, None], -1e30, 0.0).astype(bf),
        "ident_f": np.eye(P, dtype=np.float32), "ident_b": np.eye(P, dtype=bf),
        "tri": np.tile(np.tril(np.ones((NE, NE), np.float32), -1)[None], (P, 1, 1)),
    }


def kernel(**inputs):
    import concourse.bacc as _bacc
    from concourse.bass_utils import run_bass_kernel_spmd as _run

    a = {k: np.asarray(v) for k, v in inputs.items()}
    laid = {
        "x": a["L0_attn_hidden_states"].reshape(BATCH * SEQ, HID),
        "wqkv": a["L0_attn_Wqkv"], "wo": a["L0_attn_Wo"],
        "lora_a": a["L0_ffn_A"].reshape(NE * LR, HID).T,
        "lora_b": a["L0_ffn_B"].transpose(0, 2, 1).reshape(NE * LR, HID),
        "wr": a["L0_ffn_Wr"].T,
        "wq1": a["L1_attn_Wq"], "bq1": a["L1_attn_bq"],
        "wk1": a["L1_attn_Wk"].reshape(HID, HD), "bk1": a["L1_attn_bk"].reshape(HD),
        "wv1": a["L1_attn_Wv"].reshape(HID, HD), "bv1": a["L1_attn_bv"].reshape(HD),
        "gate_w": a["L1_ffn_gate_wq"].T, "gate_s": a["L1_ffn_gate_scale"].reshape(NI, P).T,
        "up_w": a["L1_ffn_up_wq"].T, "up_s": a["L1_ffn_up_scale"].reshape(NI, P).T,
        "down_w": a["L1_ffn_down_wq"].T.reshape(NI, P, HID).transpose(1, 0, 2).reshape(P, NI * HID),
        "down_s": a["L1_ffn_down_scale"],
    }
    laid.update(_constants())

    nc = _bacc.Bacc("TRN2", target_bir_lowering=False, num_devices=1)
    arrays, args = {}, []
    for name, v in laid.items():
        v = np.ascontiguousarray(v)
        arrays[f"in_{name}"] = v
        args.append(nc.dram_tensor(f"in_{name}", v.shape, mybir.dt.from_np(v.dtype), kind="ExternalInput").ap())
    args.append(nc.dram_tensor("out_y", (BATCH * SEQ, HID), F32, kind="ExternalOutput").ap())
    build(nc, *args)
    r = _run(nc, [arrays], core_ids=[0])
    return r.results[0]["out_y"].reshape(BATCH, SEQ, HID)
```

```python
import math
from contextlib import ExitStack

import numpy as np
import concourse.bass as bass
from concourse import mybir

P = 128
BATCH, SEQ, HID = 8, 256, 512
NH, HD = 32, 16
CHUNK = 512
NCH = BATCH * SEQ // CHUNK
NT = CHUNK // P
NK = HID // P
NB = CHUNK // SEQ
HG = 4
NHG = NH // HG
NE, LR = 4, 16
INTER = 1792
NI = INTER // P
EPS = 1e-5
SCALE = HD ** -0.5
LORA_SCALE = 16.0 / math.sqrt(16.0)

PART_Q = [0, 0, 1, 0, 2, 1]
PART_K = [0, 1, 0, 2, 0, 1]
R_ALIBI = 6 * HD
R_MAX = R_ALIBI + 6
ROWS = R_MAX + 3

TOKC = 2 * HD + NE + NE * LR
C_V, C_L, C_M = HD, 2 * HD, 2 * HD + NE
C1 = 3 * HD
VC = 3 * HD + 1
XS = 256.0
HS = 2.0 ** -17

U_XT, U_TOK, U_Q, U_KT, U_NM = 0, 4, 6, 10, (11, 17)
U_PV = [12, 13, 14, 15, 16, 18, 19, 20] + [21 + g for g in range(8)]
U_AT, U_OUT, UA = 29, 34, 38
F0 = [k * P for k in range(NK)] + [HID + NE * LR - P]
V_XT, V_TOK, V_GU, V_DOWN = 0, 4, 6, 6 + 2 * NI
UB = V_DOWN + NT
NSTAGE = 4
SU = 3 * NHG

F32, BF16, F16, I32 = mybir.dt.float32, mybir.dt.bfloat16, mybir.dt.float16, mybir.dt.int32
ALU = mybir.AluOpType
ACT = mybir.ActivationFunctionType
AX = mybir.AxisListType

HEAD = [("a_ln", t) for t in range(NT + 1)] + [("a_xT",), ("a_tok",), ("a_q",), ("a_kT",), ("a_gate",)]
TAIL = [("a_attT",), ("a_out", 0), ("a_out", 1), ("a_ln1", 0), ("a_out", 2), ("a_ln1", 1), ("a_out", 3),
        ("a_ln1", 2), ("a_ln1", 3), ("a_ln1", 4)]


def attention(fill):
    out = []
    for g in range(NHG):
        out += [("a_max", 0, g)] + fill()
    out += [("a_nm", 0), ("a_max", 1, 0)] + fill() + [("a_max", 1, 1)] + fill()
    last = None
    for b in range(NB):
        for g in range(NHG):
            if b == 0:
                out += [("a_max", 1, g + 2)] if g + 2 < NHG else []
                out += [("a_nm", 1)] if g + 2 == NHG else []
            out += [("a_exp", b, g)] + ([("a_pv", *last)] if last else []) + [("a_exp2", b, g)] + fill()
            out += [("a_lo", b, g)]
            last = (b, g)
    return out + [("a_pv", *last)]


GU = [(name, i) for i in range(NI) for name in ("b_gate", "b_up")]
DOWN = [(name, t) for t in range(NT) for name in ("b_half", "b_down")]
PLACES = [1] * NHG + [1, 1] + [1] * NHG + [1, 0, 1, 0, 1, 0, 0, 0] + [1]
HEAD_GU = 2 * NI + 2 * NT - sum(PLACES)


def pipelined():
    first = iter(GU[:HEAD_GU])
    rest = iter(GU[HEAD_GU:] + DOWN)
    slots = iter(PLACES)

    def gu(n):
        return [next(first) for _ in range(n)]

    def fill():
        return [next(rest) for _ in range(next(slots))]

    head = ([("b_xT",), ("a_ln", 0), ("a_ln", 1), ("b_tok",), ("a_ln", 2), ("a_ln", 3), ("a_ln", 4)] + gu(2)
            + [("a_xT",)] + gu(2) + [("a_tok",), ("a_q",)] + gu(2) + [("a_kT",), ("b_att",)] + gu(2) + [("a_gate",)]
            + gu(2) + [("b_att2",)] + gu(2) + [("b_att3",)] + list(first))
    out = head + attention(fill) + fill() + TAIL
    assert next(rest, None) is None
    return out


STAGE_A = HEAD + attention(lambda: []) + TAIL
STAGE_B = ([("b_xT",), ("b_tok",)] + GU[0:2] + [("b_att",)] + GU[2:4] + [("b_att2",)] + GU[4:6] + [("b_att3",)]
           + GU[6:] + DOWN)


def build(nc, x, wqkv, wo, lora_a, lora_b, wr, wq1, bq1, wk1, bk1, wv1, bv1,
          gate_w, gate_s, up_w, up_s, down_w, down_s, q_rows, k_cols, mask, ident_f, ident_b, tri, out):
    with ExitStack() as ctx:
        def sb(name, shape, dt):
            return ctx.enter_context(nc.sbuf_tensor(name, shape, dt))

        def sem(name):
            return ctx.enter_context(nc.semaphore(name))

        identf = sb("identf", [P, P], F32)
        identb = sb("identb", [P, P], BF16)
        maskb = sb("maskb", [P, P], BF16)
        tri_sb = sb("tri_sb", [P, NE, NE], F32)
        wq_sb = sb("wq_sb", [P, NK, HID], F32)
        wtok = sb("wtok", [P, NK, TOKC], F32)
        wo_sb = sb("wo_sb", [P, NK + 1, HID], F32)
        w48f = sb("w48f", [P, NK, C1], F32)
        w48 = sb("w48", [P, NK, 3, C1], BF16)
        bias48 = sb("bias48", [P, C1], F32)
        wgu = sb("wgu", [P, 2, NK, INTER], F16)
        wd = sb("wd", [P, NI, HID], F16)
        sg = sb("sg", [P, NI], F32)
        su = sb("su", [P, NI], F32)
        sgx = sb("sgx", [P, NI], F32)
        sux = sb("sux", [P, NI], F32)
        sprod = sb("sprod", [P, NI], F32)
        cmax = sb("cmax", [P, 4], F32)
        dsb = sb("dsb", [P, HID], F32)
        x_sb = sb("x_sb", [P, NT, HID], F32)
        attn = sb("attn", [P, NT, HID + NE * LR], F32)
        xn0 = attn[:, :, 0:HID]
        st0 = sb("st0", [P, NT, 6], F32)
        mv0 = sb("mv0", [P, NT, 2], F32)
        rs0 = sb("rs0", [P, NT], F32)
        mhalf = sb("mhalf", [P, NT], F32)
        qparts = sb("qparts", [P, 3 * NK * CHUNK], BF16)
        qs = qparts[:, :].rearrange("p (a m t) -> p a m t", a=3, m=NK)
        attnT = qparts[:, 0:5 * CHUNK * 2].bitcast(F32).rearrange("p (k t) -> p k t", k=5)
        pbuf = sb("pbuf", [P, 9 * CHUNK], F32)
        e32 = pbuf[:, 0:3 * CHUNK].rearrange("p (w t) -> p w t", w=3)
        probs = pbuf[:, 3 * CHUNK:9 * CHUNK].bitcast(F16).rearrange(
            "p (s a w t) -> p s a w t", s=2, a=2, w=3)
        xT = pbuf[:, 0:NK * CHUNK].rearrange("p (k t) -> p k t", k=NK)
        rq = pbuf[:, NK * CHUNK:(NK + 2) * CHUNK].rearrange("p (m t) -> p m t", m=2)
        kc = sb("kc", [P, NT, ROWS], BF16)
        kres = sb("kres", [P, NT, HD], F32)
        kk = sb("kk", [ROWS, NT, P], BF16)
        vv = sb("vv", [P, NT, VC], BF16)
        vres = sb("vres", [P, NT, HD], F32)
        qq = sb("qq", [ROWS, NH, CHUNK], BF16)
        mx = sb("mx", [P, NT, NH], F32)
        nres = sb("nres", [P, 2, NH], F32)
        nmp = sb("nmp", [P, NB, 2, 3, NH], BF16)
        nmT = sb("nmT", [3 * NH, NB, SEQ], BF16)
        rden = sb("rden", [P, 2 * HG], F32)
        osum = sb("osum", [P, 2 * HG, HD], F32)
        lm = sb("lm", [P, NT, NE + NE * LR], F32)
        gate = sb("gate", [P, NT, NE], F32)
        gsum = sb("gsum", [P, NT], F32)
        gmx = sb("gmx", [P, NT], F32)
        gex = sb("gex", [P, NT, NE], F32)
        gcmp = sb("gcmp", [P, NT, NE, NE], F32)
        geq = sb("geq", [P, NT, NE, NE], F32)
        grk = sb("grk", [P, NT, NE], F32)
        x1 = sb("x1", [P, NT, HID], F32)
        st1 = sb("st1", [P, NT, 6], F32)
        mv1 = sb("mv1", [P, NT, 2], F32)
        rs1 = sb("rs1", [P, NT], F32)
        hbuf = sb("hbuf", [P, 2, NI, CHUNK], F16)
        hflat = hbuf[:, :, :, :].rearrange("p a i t -> p (a i t)")
        xn1 = hflat[:, 0:NT * HID * 2].bitcast(F32).rearrange("p (t h) -> p t h", t=NT)
        S = hflat[:, NT * HID * 2:NT * (HID + HD * HD) * 2].bitcast(F32).rearrange(
            "p (t d e) -> p t d e", t=NT, d=HD)
        stage = [hflat[:, s * INTER * 2:(s + 1) * INTER * 2].bitcast(I32) for s in range(NSTAGE)]
        xs = sb("xs", [P, 2, NK, CHUNK], F16)
        wq1_st = xs[:, :, :, :].rearrange("p a k t -> p (a k t)").bitcast(F32).rearrange(
            "p (k d h) -> p k d h", k=NK, h=NH)
        t48 = sb("t48", [P, NT, C1], F32)
        kext = sb("kext", [P, 2, NT], F32)
        m1 = sb("m1", [P, 2, NT, HD], F32)
        den1 = sb("den1", [P, NT, HD], F32)
        o1 = sb("o1", [P, NT, HD], F32)
        ebuf = sb("ebuf", [P, 2, CHUNK], F32)
        hf = sb("hf", [P, 2, CHUNK], F32)
        ytmp = hf[:, 0, :]
        bq_st = ytmp.rearrange("p (d h) -> p d h", h=NH)
        w48r = hf[:, 1, 0:NK * C1].rearrange("p (k n) -> p k n", k=NK)

        def bank(name, dt=F32, n=512):
            return ctx.enter_context(nc.psum_tensor(name, [P, n], dt))

        ab = [bank("a_bank0"), bank("a_bank1")]
        bb = [bank("b_bank0"), bank("b_bank1")]
        mb = [bank("max_bank0"), bank("max_bank1")]
        eb = [bank("exp_bank0"), bank("exp_bank1")]

        s_const, s_w, s_w1 = sem("constants_loaded"), sem("weights_loaded"), sem("layer1_small_loaded")
        s_init = sem("pool_constants_set")
        s_stage = [sem(f"stage{i}_loaded") for i in range(NSTAGE)]
        s_conv = sem("ffn_weights_converted")
        s_cmax, s_call, s_wprep = sem("scale_product_ready"), sem("scale_maximum_ready"), sem("layer1_operands_ready")
        s_x = [sem(f"x_tile{t}_loaded") for t in range(NT)]
        s_var0, s_eps0, s_rs0, s_xn0 = sem("variance0"), sem("variance0_plus_eps"), sem("rstd0"), sem("xn0_ready")
        s_var1, s_eps1, s_rs1, s_xn1 = sem("variance1"), sem("variance1_plus_eps"), sem("rstd1"), sem("xn1_ready")
        a_full = [sem("a_bank0_full"), sem("a_bank1_full")]
        a_free = [sem("a_bank0_used"), sem("a_bank1_used")]
        b_full = [sem("b_bank0_full"), sem("b_bank1_full")]
        b_free = [sem("b_bank0_used"), sem("b_bank1_used")]
        m_full = [sem("max_bank0_full"), sem("max_bank1_full")]
        m_free = [sem("max_bank0_used"), sem("max_bank1_used")]
        e_full = [sem("exp_bank0_full"), sem("exp_bank1_full")]
        e_free = [sem("exp_bank0_used"), sem("exp_bank1_used")]
        s_qh, s_qm, s_qp = sem("q_high"), sem("q_middle"), sem("q_low")
        s_qd = [sem(f"q_tile{m}_in_dram") for m in range(NK)]
        s_gather, s_kc = [sem(f"q_half{i}_gathered") for i in range(2)], sem("k_columns_ready")
        s_gd, s_ge, s_gated = sem("gate_differences"), sem("gate_exp"), sem("lora_middle_gated")
        s_norm = sem("attention_normalised")
        s_nmp, s_nmrow = sem("max_parts_ready"), sem("max_rows_placed")
        s_lo01, s_lo2 = sem("probs_low_by_pool"), sem("probs_low_by_vector")
        s_xh = sem("xs_high_ready")
        s_o1, s_x1o = sem("attention1_ready"), sem("attention1_added")
        s_sd, s_se, s_att1 = sem("scores1_ready"), sem("scores1_exp"), sem("attention1_done")
        s_sig, s_hh, s_hl = sem("gate_exp1"), sem("h_high_ready"), sem("h_low_ready")
        s_y = sem("y_ready")
        s_out = [sem(f"y_tile{t}_stored") for t in range(NT)]
        s_held = sem("waits_held")
        d_w, d_a, d_b = sem("vector_setup_chain"), sem("vector_a_chain"), sem("vector_b_chain")

        def wait(eng, s, v):
            if not (isinstance(v, int) and v <= 0):
                eng.wait_ge(s, v)

        def hold(eng):
            eng.sem_inc(s_held, 1)

        def wait_full(eng, full, u, c, per):
            eng.wait_ge(full[u % 2], c * (per // 2) + (u // 2 + 1))

        def wait_free(eng, free, u, c, per):
            wait(eng, free[u % 2], c * (per // 2) + u // 2 + (free is b_free))

        def wait_used(eng, free, u, c, per):
            eng.wait_ge(free[u % 2], c * (per // 2) + (u // 2 + 1 + (free is b_free)))

        def run(eng, steps, chains=()):
            def do(names, ca, cb):
                for name in names:
                    if name[0] in steps:
                        steps[name[0]](ca if name[0][0] == "a" else cb, *name[1:])

            do(STAGE_A, 0, None)
            for ch in chains:
                ch.close()
            with eng.Fori(1, NCH) as c:
                do(pipelined(), c, c - 1)
                for ch in chains:
                    ch.close()
            do(STAGE_B, None, NCH - 1)

        class Chain:

            def __init__(self, eng, s, per):
                self.eng, self.s, self.per, self.n = eng, s, per, 0

            def link(self, c, ins):
                self.n += 1
                ins.then_inc(self.s, 1)
                self.eng.wait_ge(self.s, c * self.per + self.n)

            def close(self):
                assert self.n in (0, self.per), (self.n, self.per)
                self.n = 0

        x_v = x.rearrange("(c t p) h -> c p t h", p=P, t=NT)
        out_v = out.rearrange("(c t p) h -> c p t h", p=P, t=NT)
        q_dram = nc.dram_tensor("q_parts", [3, NH * HD, CHUNK], BF16).ap()

        block = ctx.enter_context(nc.Block())

        constants = [(identf[:, :], ident_f), (identb[:, :], ident_b), (maskb[:, :], mask), (tri_sb[:, :, :], tri),
                     (kc[:, :, R_ALIBI:ROWS], k_cols), (qq[R_ALIBI:R_MAX, :, :], q_rows)]
        kp = "(k p) n -> p k n"
        weights = [(wq_sb[:, :, :], wqkv[:, 0:HID].rearrange(kp, p=P)),
                   (wtok[:, :, 0:C_L], wqkv[:, HID:HID + 2 * HD].rearrange(kp, p=P)),
                   (wtok[:, :, C_L:C_M], wr.rearrange(kp, p=P)),
                   (wtok[:, :, C_M:TOKC], lora_a.rearrange(kp, p=P)),
                   (wo_sb[:, 0:NK, :], wo.rearrange(kp, p=P)),
                   (wo_sb[P - NE * LR:P, NK, :], lora_b)]
        layer1_small = [(wq1_st, wq1.rearrange("(k p) d h -> p k d h", p=P)),
                        (bq_st, bq1.partition_broadcast(P)),
                        (bias48[:, HD:2 * HD], bk1.partition_broadcast(P)),
                        (bias48[:, 2 * HD:C1], bv1.partition_broadcast(P)),
                        (w48f[:, :, HD:2 * HD], wk1.rearrange(kp, p=P)),
                        (w48f[:, :, 2 * HD:C1], wv1.rearrange(kp, p=P)),
                        (sg[:, :], gate_s), (su[:, :], up_s), (dsb[:, :], down_s.partition_broadcast(P))]
        wd_flat = wd[:, :, :].rearrange("p i n -> p (i n)")
        pieces = ([(wgu[:, 0, k, :], gate_w[k * P:(k + 1) * P, :]) for k in range(NK)]
                  + [(wgu[:, 1, k, :], up_w[k * P:(k + 1) * P, :]) for k in range(NK)]
                  + [(wd_flat[:, q * INTER:(q + 1) * INTER], down_w[:, q * INTER:(q + 1) * INTER])
                     for q in range(NI * HID // INTER)])
        N_GATHER = len(PART_Q)

        @block.sync
        def _(sp):
            def a_ln(c, t):
                if t < NT:
                    if not isinstance(c, int):
                        wait_used(sp, a_free, U_OUT + t, c - 1, UA)
                    sp.dma_start(x_sb[:, t, :], x_v[c][:, t, :]).then_inc(s_x[t], 16)
                if isinstance(c, int) and t == NT:
                    for dst, src in constants:
                        sp.dma_start(dst, src).then_inc(s_const, 16)
                    for dst, src in weights:
                        sp.dma_start(dst, src).then_inc(s_w, 16)
                    for dst, src in layer1_small:
                        sp.dma_start(dst, src).then_inc(s_w1, 16)

            def a_q(c):
                for m in range(NK):
                    sp.wait_ge(s_qp, c * NK + m + 1)
                    sp.dma_start(q_dram[:, m * P:(m + 1) * P, :].rearrange("a r t -> r a t"),
                                 qs[:, :, m, :]).then_inc(s_qd[m], 16)
                for half in range(2):
                    for m in (2 * half, 2 * half + 1):
                        sp.wait_ge(s_qd[m], 16 * (c + 1))
                    hs = slice(half * NH // 2, (half + 1) * NH // 2)
                    for g, part in enumerate(PART_Q):
                        sp.dma_start(qq[HD * g:HD * g + HD, hs, :],
                                     q_dram[part].rearrange("(h d) t -> d h t", d=HD)[:, hs, :])\
                          .then_inc(s_gather[half], 16)

            def a_nm(c, b):
                wait_used(sp, a_free, U_NM[b], c, UA)
                for part in range(3):
                    sp.dma_start(qq[R_MAX + part:R_MAX + part + 1, :, b * SEQ:(b + 1) * SEQ],
                                 nmT[part * NH:(part + 1) * NH, b, :]).then_inc(s_nmrow, 16)

            def b_down(c, t):
                sp.wait_ge(s_y, c * NT + t + 1)
                sp.dma_start(out_v[c][:, t, :], x1[:, t, :]).then_inc(s_out[t], 16)

            run(sp, {"a_ln": a_ln, "a_q": a_q, "a_nm": a_nm, "b_down": b_down})
            for t in range(NT):
                sp.wait_ge(s_out[t], 16 * NCH)

        @block.gpsimd
        def _(pool):
            pool.memset(mhalf[:, :], -0.5).then_inc(s_init, 1)
            pool.memset(vv[:, :, 3 * HD:VC], 1.0).then_inc(s_init, 1)
            pool.memset(wo_sb[0:P - NE * LR, NK, :], 0.0).then_inc(s_init, 1)

            def load_piece(n):
                wait(pool, s_conv, n - NSTAGE + 1)
                pool.dma_start(stage[n % NSTAGE], pieces[n][1]).then_inc(s_stage[n % NSTAGE], 16)

            def rstd(c, t, s_var, mv, rs, s_eps, s_rs):
                pool.wait_ge(s_var, c * NT + t + 1)
                hold(pool)
                pool.tensor_scalar(rs[:, t:t + 1], mv[:, t, 1:2], EPS, None, ALU.add).then_inc(s_eps, 1)
                pool.wait_ge(s_eps, c * NT + t + 1)
                pool.tensor_tensor(rs[:, t:t + 1], rs[:, t:t + 1], mhalf[:, t:t + 1], ALU.pow).then_inc(s_rs, 1)

            def a_ln(c, t):
                if isinstance(c, int) and t == 0:
                    for n in range(NSTAGE):
                        load_piece(n)
                    pool.wait_ge(s_init, 3)
                if t < NT:
                    rstd(c, t, s_var0, mv0, rs0, s_eps0, s_rs0)

            def a_max(c, b, g):
                n = b * NHG + g + NSTAGE
                if isinstance(c, int) and n < len(pieces):
                    load_piece(n)

            def a_nm(c, b):
                if isinstance(c, int) and b == 0:
                    pool.wait_ge(s_cmax, 1)
                    pool.partition_all_reduce(cmax[:, 1:2], cmax[:, 0:1], P,
                                              bass.bass_isa.ReduceOp.max).then_inc(s_call, 1)

            def a_q(c):
                for m in range(NK):
                    wait_used(pool, a_free, U_Q + m, c, UA)
                    hold(pool)
                    pool.tensor_scalar(qs[:, 1, m, :], rq[:, m % 2, :], 1.0, None, ALU.mult).then_inc(s_qm, 1)
                    pool.wait_ge(s_qm, c * NK + m + 1)
                    pool.tensor_tensor(qs[:, 2, m, :], rq[:, m % 2, :], qs[:, 1, m, :], ALU.subtract)\
                        .then_inc(s_qp, 1)

            def a_exp(c, b, g):
                n = b * NHG + g
                for w in (0, 1):
                    wait_used(pool, e_free, 3 * n + w, c, NB * SU)
                    pool.tensor_tensor(probs[:, n % 2, 1, w, :], e32[:, w, :], probs[:, n % 2, 0, w, :],
                                       ALU.subtract).then_inc(s_lo01, 1)

            def b_att3(c):
                pool.wait_ge(s_o1, c + 1)
                x1v = x1[:, :, :].rearrange("p t (d h) -> p t d h", h=NH)
                pool.tensor_tensor(x1v, x1v, o1[:, :, :].unsqueeze(3).broadcast_to([P, NT, HD, NH]),
                                   ALU.add).then_inc(s_x1o, 1)

            def a_ln1(c, t):
                if t < NT:
                    rstd(c, t, s_var1, mv1, rs1, s_eps1, s_rs1)

            def h_low(c, i):
                pool.wait_ge(s_hh, c * NI + i + 1)
                pool.tensor_tensor(hbuf[:, 1, i, :], hf[:, i % 2, :], hbuf[:, 0, i, :],
                                   ALU.subtract).then_inc(s_hl, 1)

            def b_up(c, i):
                if i:
                    h_low(c, i - 1)

            def b_half(c, t):
                if t == 0:
                    h_low(c, NI - 1)

            run(pool, {"a_ln": a_ln, "a_q": a_q, "a_max": a_max, "a_nm": a_nm, "a_exp": a_exp,
                       "a_ln1": a_ln1, "b_att3": b_att3, "b_up": b_up, "b_half": b_half})

        @block.scalar
        def _(act):
            def a_xT(c):
                for k in range(NK):
                    u = U_XT + k
                    wait_full(act, a_full, u, c, UA)
                    act.activation(xT[:, k, :], ab[u % 2][:, :], ACT.Copy).then_inc(a_free[u % 2], 1)

            def a_q(c):
                for m in range(NK):
                    u = U_Q + m
                    wait_full(act, a_full, u, c, UA)
                    act.activation(qs[:, 0, m, :], ab[u % 2][:, :], ACT.Copy, scale=SCALE).then_inc(s_qh, 1)

            def a_kT(c):
                wait_full(act, a_full, U_KT, c, UA)
                act.activation(kk[:, :, :].rearrange("r t p -> r (t p)"),
                               ab[U_KT % 2][0:ROWS, 0:NT * P // 2].bitcast(BF16), ACT.Copy)\
                   .then_inc(a_free[U_KT % 2], 1)

            def a_max(c, b, g):
                n = b * NHG + g
                if isinstance(c, int) and n < len(pieces):
                    act.wait_ge(s_stage[n % NSTAGE], 16 * (n // NSTAGE + 1))
                    act.activation(pieces[n][0], stage[n % NSTAGE], ACT.Copy).then_inc(s_conv, 1)

            def a_gate(c):
                act.wait_ge(s_gd, c + 1)
                act.activation(gex[:, :, :], gex[:, :, :], ACT.Exp).then_inc(s_ge, 1)

            def a_nm(c, b):
                u = U_NM[b]
                wait_full(act, a_full, u, c, UA)
                act.activation(nmT[:, b, :], ab[u % 2][0:3 * NH, 0:SEQ // 2].bitcast(BF16), ACT.Copy)\
                   .then_inc(a_free[u % 2], 1)

            def exp(c, n, w):
                if n and w < 2:
                    act.wait_ge(s_lo01, 2 * (c * NB * NHG + n) - 1 + w)
                elif n:
                    act.wait_ge(s_lo2, c * NB * NHG + n)
                if n >= 2 and w == 0:
                    wait_full(act, a_full, U_PV[n - 2], c, UA)
                u = n * 3 + w
                wait_full(act, e_full, u, c, NB * SU)
                act.activation(e32[:, w, :], eb[u % 2][:, :], ACT.Exp)
                act.activation(probs[:, n % 2, 0, w, :], eb[u % 2][:, :], ACT.Exp).then_inc(e_free[u % 2], 1)

            def a_exp(c, b, g):
                for w in range(2):
                    exp(c, b * NHG + g, w)

            def a_exp2(c, b, g):
                exp(c, b * NHG + g, 2)

            def a_attT(c):
                for k in range(NK + 1):
                    u = U_AT + k
                    wait_full(act, a_full, u, c, UA)
                    act.activation(attnT[:, k, :], ab[u % 2][:, :], ACT.Copy).then_inc(a_free[u % 2], 1)

            def b_xT(c):
                for k in range(NK):
                    u = V_XT + k
                    wait_full(act, b_full, u, c, UB)
                    act.activation(xs[:, 0, k, :], bb[u % 2][:, :], ACT.Copy, scale=XS).then_inc(s_xh, 1)

            def b_att(c):
                act.wait_ge(s_sd, c + 1)
                act.activation(S, S, ACT.Exp, scale=SCALE).then_inc(s_se, 1)

            def h_high(c, i):
                wait_used(act, b_free, V_GU + 2 * i + 1, c, UB)
                act.activation(hbuf[:, 0, i, :], hf[:, i % 2, :], ACT.Copy).then_inc(s_hh, 1)

            def b_gate(c, i):
                u = V_GU + 2 * i
                if i == 0:
                    act.wait_ge(s_wprep, 1)
                if i == 8:
                    act.wait_ge(s_att1, c + 1)
                wait_full(act, b_full, u, c, UB)
                if i >= 2:
                    wait_used(act, b_free, V_GU + 2 * (i - 2) + 1, c, UB)
                act.activation(ebuf[:, i % 2, :], bb[u % 2][:, :], ACT.Tanh, scale=sgx[:, i:i + 1])\
                   .then_inc(s_sig, 1)
                if i:
                    h_high(c, i - 1)

            def b_half(c, t):
                if t == 0:
                    h_high(c, NI - 1)

            run(act, {"a_xT": a_xT, "a_q": a_q, "a_kT": a_kT, "a_gate": a_gate, "a_max": a_max, "a_nm": a_nm,
                      "a_exp": a_exp, "a_exp2": a_exp2, "a_attT": a_attT, "b_xT": b_xT, "b_att": b_att,
                      "b_gate": b_gate, "b_half": b_half})

        @block.tensor
        def _(pe):
            def a_xT(c):
                if isinstance(c, int):
                    pe.wait_ge(s_const, 16 * len(constants))
                pe.wait_ge(s_xn0, c * NT + NT)
                for k in range(NK):
                    u = U_XT + k
                    wait_free(pe, a_free, u, c, UA)
                    for t in range(NT):
                        mm = pe.transpose(ab[u % 2][:, t * P:(t + 1) * P], xn0[:, t, k * P:(k + 1) * P],
                                          identf[:, :])
                    mm.then_inc(a_full[u % 2], 1)

            def a_tok(c):
                if isinstance(c, int):
                    pe.wait_ge(s_w, 16 * len(weights))
                for k in (NK - 2, NK - 1):
                    wait_used(pe, a_free, U_XT + k, c, UA)
                for w in range(2):
                    u = U_TOK + w
                    wait_free(pe, a_free, u, c, UA)
                    for t in (0, 1):
                        for k in range(NK):
                            mm = pe.matmul(ab[u % 2][:, t * TOKC:(t + 1) * TOKC],
                                           xT[:, k, (2 * w + t) * P:(2 * w + t + 1) * P], wtok[:, k, :],
                                           start=(k == 0), stop=(k == NK - 1))
                    mm.then_inc(a_full[u % 2], 1)

            def a_kT(c):
                pe.wait_ge(s_kc, c * 2 + 2)
                wait_free(pe, a_free, U_KT, c, UA)
                kb = ab[U_KT % 2][0:ROWS, 0:NT * P // 2].bitcast(BF16)
                for t in range(NT):
                    mm = pe.transpose(kb[:, t * P:(t + 1) * P], kc[:, t, :], identb[:, :])
                mm.then_inc(a_full[U_KT % 2], 1)

            def a_q(c):
                for m in range(NK):
                    u = U_Q + m
                    wait_free(pe, a_free, u, c, UA)
                    for k in range(NK):
                        mm = pe.matmul(ab[u % 2][:, :], wq_sb[:, k, m * P:(m + 1) * P], xT[:, k, :],
                                       start=(k == 0), stop=(k == NK - 1))
                    mm.then_inc(a_full[u % 2], 1)

            def a_max(c, b, g):
                n = b * NHG + g
                q0 = b * SEQ
                if n == 0:
                    wait_used(pe, a_free, U_KT, c, UA)
                if n in (0, NHG // 2):
                    pe.wait_ge(s_gather[n // (NHG // 2)], 16 * N_GATHER * (c + 1))
                for w in range(3):
                    u = 3 * n + w
                    bank = mb[u % 2]
                    wait_free(pe, m_free, u, c, NB * SU)
                    if w == 0:
                        pe.matmul(bank[:, :].rearrange("p (h k) -> p h k", h=HG), identb[:, :],
                                  maskb[:, :].unsqueeze(1).broadcast_to([P, HG, P]), start=True, stop=False,
                                  skip_group_check=True)
                        for j in range(HG):
                            mm = pe.matmul(bank[:, j * P:(j + 1) * P],
                                           qq[0:R_MAX, HG * g + j, q0:q0 + P], kk[0:R_MAX, 2 * b, :],
                                           start=False, stop=True, skip_group_check=True)
                    else:
                        pe.matmul(bank[:, :].rearrange("p (h k) -> p h k", h=2)[:, :, P:SEQ], identb[:, :],
                                  maskb[:, :].unsqueeze(1).broadcast_to([P, 2, P]), start=True, stop=False,
                                  skip_group_check=True)
                        for j in range(2):
                            mm = pe.matmul(bank[:, j * SEQ:(j + 1) * SEQ],
                                           qq[0:R_MAX, HG * g + 2 * (w - 1) + j, q0 + P:q0 + SEQ],
                                           kk[0:R_MAX, 2 * b:2 * b + 2, :].rearrange("r t p -> r (t p)"),
                                           start=False, stop=True, skip_group_check=True)
                    mm.then_inc(m_full[u % 2], 1)

            def a_nm(c, b):
                u = U_NM[b]
                pe.wait_ge(s_nmp, c * NB + b + 1)
                wait_free(pe, a_free, u, c, UA)
                nb = ab[u % 2][0:3 * NH, 0:SEQ // 2].bitcast(BF16)
                for t in range(2):
                    mm = pe.transpose(nb[:, t * P:(t + 1) * P],
                                      nmp[:, b, t, :, :].rearrange("p a h -> p (a h)"), identb[:, :])
                mm.then_inc(a_full[u % 2], 1)

            def a_exp(c, b, g):
                if g == 0:
                    pe.wait_ge(s_nmrow, 48 * (c * NB + b + 1))
                for w in range(2):
                    scores(c, b, g, w)

            def a_exp2(c, b, g):
                scores(c, b, g, 2)

            def scores(c, b, g, w):
                u = 3 * (b * NHG + g) + w
                wait_free(pe, e_free, u, c, NB * SU)
                kt, qt = ((0, 0), (0, 1), (1, 1))[w]
                if kt == qt:
                    pe.matmul(eb[u % 2][:, :].rearrange("p (h q) -> p h q", h=HG), maskb[:, :],
                              identb[:, :].unsqueeze(1).broadcast_to([P, HG, P]), start=True, stop=False)
                pe.matmul(eb[u % 2][:, :], kk[0:ROWS, 2 * b + kt, :],
                          qq[0:ROWS, HG * g:HG * g + HG, b * SEQ + qt * P:b * SEQ + (qt + 1) * P],
                          start=(kt != qt), stop=True).then_inc(e_full[u % 2], 1)

            def a_pv(c, b, g):
                n = b * NHG + g
                u = U_PV[n]
                wait_free(pe, a_free, u, c, UA)
                pe.wait_ge(s_lo01, 2 * (c * NB * NHG + n + 1))
                pe.wait_ge(s_lo2, c * NB * NHG + n + 1)
                pvb = ab[u % 2][:, 0:2 * HG * VC].rearrange("p (t h d) -> p t h d", t=2, h=HG)
                for j in range(HG):
                    for qt, pairs in ((0, [(0, 0)]), (1, [(1, 0), (2, 1)])):
                        for w, kt in pairs:
                            for part in (0, 1):
                                mm = pe.matmul(pvb[:, qt, j, :], probs[:, n % 2, part, w, j * P:(j + 1) * P],
                                               vv[:, 2 * b + kt, :], start=(kt == 0 and part == 0),
                                               stop=(kt == qt and part == 1))
                mm.then_inc(a_full[u % 2], 1)

            def a_attT(c):
                pe.wait_ge(s_gated, c + 1)
                pe.wait_ge(s_norm, NB * NHG * (c + 1))
                for k in range(NK + 1):
                    u = U_AT + k
                    wait_free(pe, a_free, u, c, UA)
                    for t in range(NT):
                        mm = pe.transpose(ab[u % 2][:, t * P:(t + 1) * P], attn[:, t, F0[k]:F0[k] + P],
                                          identf[:, :])
                    mm.then_inc(a_full[u % 2], 1)

            def a_out(c, t):
                if t == 0:
                    for k in (NK - 1, NK):
                        wait_used(pe, a_free, U_AT + k, c, UA)
                u = U_OUT + t
                wait_free(pe, a_free, u, c, UA)
                for k in range(NK + 1):
                    mm = pe.matmul(ab[u % 2][:, :], attnT[:, k, t * P:(t + 1) * P], wo_sb[:, k, :],
                                   start=(k == 0), stop=(k == NK))
                mm.then_inc(a_full[u % 2], 1)

            def b_xT(c):
                pe.wait_ge(s_xn1, c * NT + NT)
                for k in range(NK):
                    u = V_XT + k
                    wait_free(pe, b_free, u, c, UB)
                    for t in range(NT):
                        mm = pe.transpose(bb[u % 2][:, t * P:(t + 1) * P], xn1[:, t, k * P:(k + 1) * P],
                                          identf[:, :])
                    mm.then_inc(b_full[u % 2], 1)

            def b_tok(c):
                for k in (NK - 2, NK - 1):
                    wait_used(pe, b_free, V_XT + k, c, UB)
                pe.wait_ge(s_wprep, 1)
                for w in range(2):
                    u = V_TOK + w
                    wait_free(pe, b_free, u, c, UB)
                    for t in (0, 1):
                        for k in range(NK):
                            for part in (0, 1):
                                mm = pe.matmul(bb[u % 2][:, t * 3 * C1:(t + 1) * 3 * C1],
                                               xs[:, part, k, (2 * w + t) * P:(2 * w + t + 1) * P],
                                               w48[:, k, :, :].rearrange("p a n -> p (a n)"),
                                               start=(k == 0 and part == 0), stop=(k == NK - 1 and part == 1))
                    mm.then_inc(b_full[u % 2], 1)

            def gate_or_up(c, i, m):
                u = V_GU + 2 * i + m
                wait_free(pe, b_free, u, c, UB)
                for k in range(NK):
                    for part in (0, 1):
                        mm = pe.matmul(bb[u % 2][:, :], wgu[:, m, k, i * P:(i + 1) * P], xs[:, part, k, :],
                                       start=(k == 0 and part == 0), stop=(k == NK - 1 and part == 1))
                mm.then_inc(b_full[u % 2], 1)

            def b_gate(c, i):
                if i == 0:
                    pe.wait_ge(s_conv, 3 * NK)
                gate_or_up(c, i, 0)

            def b_up(c, i):
                gate_or_up(c, i, 1)

            def down(c, t, tiles):
                u = V_DOWN + t
                for i in tiles:
                    if t == 0:
                        pe.wait_ge(s_hl, c * NI + i + 1)
                    for part in (0, 1):
                        mm = pe.matmul(bb[u % 2][:, :], hbuf[:, part, i, t * P:(t + 1) * P], wd[:, i, :],
                                       start=(i == 0 and part == 0), stop=(i == NI - 1 and part == 1))
                return mm

            def b_half(c, t):
                wait_free(pe, b_free, V_DOWN + t, c, UB)
                down(c, t, range(NI // 2))

            def b_down(c, t):
                down(c, t, range(NI // 2, NI)).then_inc(b_full[(V_DOWN + t) % 2], 1)

            run(pe, {"a_xT": a_xT, "a_tok": a_tok, "a_kT": a_kT, "a_q": a_q, "a_max": a_max, "a_nm": a_nm,
                     "a_exp": a_exp, "a_exp2": a_exp2, "a_pv": a_pv, "a_attT": a_attT, "a_out": a_out,
                     "b_xT": b_xT, "b_tok": b_tok, "b_gate": b_gate, "b_up": b_up, "b_half": b_half,
                     "b_down": b_down})

        @block.vector
        def _(dve):
            ca = Chain(dve, d_a, 33)
            cb = Chain(dve, d_b, 7)
            for s in b_free:
                dve.sem_inc(s, 1)

            def layernorm(c, t, xin, st, mv, s_var, rs, s_rs, xn, s_xn, ch):
                if t < NT:
                    ch.link(c, dve.bn_stats(st[:, t, :], xin[:, t, :]))
                    hold(dve)
                    dve.bn_aggr(mv[:, t, :], st[:, t, :]).then_inc(s_var, 1)
                if t:
                    dve.wait_ge(s_rs, c * NT + t)
                    dve.tensor_scalar(xn[:, t - 1, :], xin[:, t - 1, :], mv[:, t - 1, 0:1], rs[:, t - 1:t],
                                      ALU.subtract, ALU.mult).then_inc(s_xn, 1)

            def a_ln(c, t):
                if t < NT:
                    dve.wait_ge(s_x[t], 16 * (c + 1))
                layernorm(c, t, x_sb, st0, mv0, s_var0, rs0, s_rs0, xn0, s_xn0, ca)

            def a_ln1(c, t):
                if t < NT:
                    wait_used(dve, a_free, U_OUT + t, c, UA)
                layernorm(c, t, x1, st1, mv1, s_var1, rs1, s_rs1, xn1, s_xn1, ca)

            def a_tok(c):
                if isinstance(c, int):
                    dve.wait_ge(s_const, 16 * len(constants))
                for w in range(2):
                    u = U_TOK + w
                    ts = slice(2 * w, 2 * w + 2)
                    tok = ab[u % 2][:, 0:2 * TOKC].rearrange("p (t n) -> p t n", t=2)
                    wait_full(dve, a_full, u, c, UA)
                    dve.tensor_copy(lm[:, ts, :], tok[:, :, C_L:TOKC])
                    ca.link(c, dve.tensor_copy(vv[:, ts, 0:HD], tok[:, :, C_V:C_L]))
                    ca.link(c, dve.tensor_tensor(vres[:, ts, :], tok[:, :, C_V:C_L], vv[:, ts, 0:HD], ALU.subtract))
                    ca.link(c, dve.tensor_copy(vv[:, ts, HD:2 * HD], vres[:, ts, :]))
                    dve.tensor_tensor(vv[:, ts, 2 * HD:3 * HD], vres[:, ts, :], vv[:, ts, HD:2 * HD], ALU.subtract)
                    kg = kc[:, ts, 0:R_ALIBI].rearrange("p t (g d) -> p t g d", d=HD)
                    ca.link(c, dve.tensor_copy(kg[:, :, 0:5:2, :],
                                               tok[:, :, 0:HD].unsqueeze(2).broadcast_to([P, 2, 3, HD])))
                    dve.tensor_tensor(kres[:, ts, :], tok[:, :, 0:HD], kg[:, :, 0, :],
                                      ALU.subtract).then_inc(a_free[u % 2], 1)
                    wait_used(dve, a_free, u, c, UA)
                    ca.link(c, dve.tensor_copy(kg[:, :, 1:6:4, :],
                                               kres[:, ts, :].unsqueeze(2).broadcast_to([P, 2, 2, HD])))
                    dve.tensor_tensor(kg[:, :, 3, :], kres[:, ts, :], kg[:, :, 1, :],
                                      ALU.subtract).then_inc(s_kc, 1)

            def a_q(c):
                for m in range(NK):
                    u = U_Q + m
                    dve.wait_ge(s_qh, c * NK + m + 1)
                    if m >= 2:
                        dve.wait_ge(s_qp, c * NK + m - 1)
                    dve.scalar_tensor_tensor(out=rq[:, m % 2, :], in0=ab[u % 2][:, :], scalar=SCALE,
                                             in1=qs[:, 0, m, :], op0=ALU.mult,
                                             op1=ALU.subtract).then_inc(a_free[u % 2], 1)

            def a_gate(c):
                lg = lm[:, :, 0:NE]
                dve.wait_ge(s_kc, c * 2 + 2)
                ca.link(c, dve.tensor_reduce(gmx[:, :], lg, AX.X, ALU.max))
                dve.tensor_tensor(gex[:, :, :], lg, gmx[:, :].unsqueeze(2).broadcast_to([P, NT, NE]),
                                  ALU.subtract).then_inc(s_gd, 1)
                li = lg.unsqueeze(3).broadcast_to([P, NT, NE, NE])
                lj = lg.unsqueeze(2).broadcast_to([P, NT, NE, NE])
                dve.tensor_tensor(gcmp[:, :, :, :], lj, li, ALU.is_gt)
                ca.link(c, dve.tensor_tensor(geq[:, :, :, :], lj, li, ALU.is_equal))
                ca.link(c, dve.tensor_tensor(geq[:, :, :, :], geq[:, :, :, :],
                                             tri_sb[:, :, :].unsqueeze(1).broadcast_to([P, NT, NE, NE]), ALU.mult))
                ca.link(c, dve.tensor_tensor(gcmp[:, :, :, :], gcmp[:, :, :, :], geq[:, :, :, :], ALU.add))
                ca.link(c, dve.tensor_reduce(grk[:, :, :], gcmp[:, :, :, :], AX.X, ALU.add))
                dve.wait_ge(s_ge, c + 1)
                ca.link(c, dve.scalar_tensor_tensor(out=gate[:, :, :], in0=grk[:, :, :], scalar=2.0,
                                                    in1=gex[:, :, :], op0=ALU.is_lt, op1=ALU.mult))
                ca.link(c, dve.tensor_reduce(gsum[:, :], gate[:, :, :], AX.X, ALU.add))
                ca.link(c, dve.reciprocal(gsum[:, :], gsum[:, :]))
                ca.link(c, dve.scalar_tensor_tensor(out=gate[:, :, :], in0=gate[:, :, :], scalar=LORA_SCALE,
                                                    in1=gsum[:, :].unsqueeze(2).broadcast_to([P, NT, NE]),
                                                    op0=ALU.mult, op1=ALU.mult))
                dve.tensor_tensor(attn[:, :, HID:HID + NE * LR].rearrange("p t (e r) -> p t e r", e=NE),
                                  lm[:, :, NE:NE + NE * LR].rearrange("p t (e r) -> p t e r", e=NE),
                                  gate[:, :, :].unsqueeze(3).broadcast_to([P, NT, NE, LR]),
                                  ALU.mult).then_inc(s_gated, 1)
                if isinstance(c, int):
                    setup()

            def setup():
                n = [0]

                def link(ins):
                    n[0] += 1
                    ins.then_inc(d_w, 1)
                    dve.wait_ge(d_w, n[0])

                dve.wait_ge(s_w1, 16 * len(layer1_small))
                link(dve.tensor_tensor(sprod[:, :], sg[:, :], su[:, :], ALU.mult))
                link(dve.scalar_tensor_tensor(out=sprod[:, :], in0=sprod[:, :], scalar=-1.0, in1=sprod[:, :],
                                              op0=ALU.mult, op1=ALU.max))
                dve.tensor_reduce(cmax[:, 0:1], sprod[:, :], AX.X, ALU.max).then_inc(s_cmax, 1)
                link(dve.tensor_reduce(w48f[:, :, 0:HD], wq1_st, AX.X, ALU.add))
                link(dve.tensor_reduce(bias48[:, 0:HD], bq_st, AX.X, ALU.add))
                link(dve.tensor_copy(w48[:, :, 0, :], w48f[:, :, :]))
                link(dve.tensor_tensor(w48r, w48f[:, :, :], w48[:, :, 0, :], ALU.subtract))
                link(dve.tensor_copy(w48[:, :, 1, :], w48r))
                link(dve.tensor_tensor(w48[:, :, 2, :], w48r, w48[:, :, 1, :], ALU.subtract))
                dve.tensor_scalar(sgx[:, :], sg[:, :], 0.5 / XS, None, ALU.mult)
                dve.wait_ge(s_call, 1)
                link(dve.tensor_scalar(cmax[:, 2:3], cmax[:, 1:2], 1e-30, None, ALU.max))
                link(dve.reciprocal(cmax[:, 3:4], cmax[:, 2:3]))
                link(dve.tensor_scalar(sux[:, :], su[:, :], cmax[:, 3:4], HS / XS, ALU.mult, ALU.mult))
                link(dve.tensor_tensor(sux[:, :], sux[:, :], sgx[:, :], ALU.mult))
                dve.tensor_scalar(dsb[:, :], dsb[:, :], cmax[:, 2:3], 1.0 / HS, ALU.mult,
                                  ALU.mult).then_inc(s_wprep, 1)

            def a_max(c, b, g):
                n = b * NHG + g
                for w in range(3):
                    u = 3 * n + w
                    wait_full(dve, m_full, u, c, NB * SU)
                    h0 = HG * g + (0 if w == 0 else 2 * (w - 1))
                    nh, nk = (HG, P) if w == 0 else (2, SEQ)
                    dve.tensor_reduce(mx[:, 2 * b + (w > 0), h0:h0 + nh],
                                      mb[u % 2][:, :].rearrange("p (h k) -> p h k", k=nk), AX.X,
                                      ALU.max).then_inc(m_free[u % 2], 1)

            def a_nm(c, b):
                for u in (SU * (b + 1) - 2, SU * (b + 1) - 1):
                    wait_used(dve, m_free, u, c, NB * SU)
                mv = mx[:, 2 * b:2 * b + 2, :]
                ca.link(c, dve.tensor_scalar(nmp[:, b, :, 0, :], mv, -1.0, None, ALU.mult))
                ca.link(c, dve.scalar_tensor_tensor(out=nres[:, :, :], in0=mv, scalar=-1.0, in1=nmp[:, b, :, 0, :],
                                                    op0=ALU.mult, op1=ALU.subtract))
                ca.link(c, dve.tensor_copy(nmp[:, b, :, 1, :], nres[:, :, :]))
                dve.tensor_tensor(nmp[:, b, :, 2, :], nres[:, :, :], nmp[:, b, :, 1, :],
                                  ALU.subtract).then_inc(s_nmp, 1)

            def a_lo(c, b, g):
                n = b * NHG + g
                wait_used(dve, e_free, 3 * n + 2, c, NB * SU)
                dve.tensor_tensor(probs[:, n % 2, 1, 2, :], e32[:, 2, :], probs[:, n % 2, 0, 2, :],
                                  ALU.subtract).then_inc(s_lo2, 1)

            def a_pv(c, b, g):
                n = b * NHG + g
                u = U_PV[n]
                wait_full(dve, a_full, u, c, UA)
                pvb = ab[u % 2][:, 0:2 * HG * VC].rearrange("p (n d) -> p n d", d=VC)
                if n:
                    dve.wait_ge(s_norm, c * NB * NHG + n)
                dve.tensor_reduce(osum[:, :, :], pvb[:, :, 0:3 * HD].rearrange("p n (a d) -> p n d a", a=3),
                                  AX.X, ALU.add)
                dve.reciprocal(rden[:, :], pvb[:, :, 3 * HD]).then_inc(a_free[u % 2], 1)
                wait_used(dve, a_free, u, c, UA)
                h0 = HG * g * HD
                dve.tensor_tensor(attn[:, 2 * b:2 * b + 2, h0:h0 + HG * HD].rearrange("p t (h d) -> p t h d", d=HD),
                                  osum[:, :, :].rearrange("p (t h) d -> p t h d", t=2),
                                  rden[:, :].rearrange("p (t h) -> p t h", t=2).unsqueeze(3)
                                  .broadcast_to([P, 2, HG, HD]), ALU.mult).then_inc(s_norm, 1)

            def a_out(c, t):
                wait(dve, s_out[t], 16 * c)
                u = U_OUT + t
                wait_full(dve, a_full, u, c, UA)
                dve.tensor_tensor(x1[:, t, :], ab[u % 2][:, :], x_sb[:, t, :],
                                  ALU.add).then_inc(a_free[u % 2], 1)

            def b_xT(c):
                for k in range(NK):
                    u = V_XT + k
                    dve.wait_ge(s_xh, c * NK + k + 1)
                    dve.scalar_tensor_tensor(out=xs[:, 1, k, :], in0=bb[u % 2][:, :], scalar=XS,
                                             in1=xs[:, 0, k, :], op0=ALU.mult,
                                             op1=ALU.subtract).then_inc(b_free[u % 2], 1)

            def b_tok(c):
                for w in range(2):
                    u = V_TOK + w
                    wait_full(dve, b_full, u, c, UB)
                    dve.tensor_reduce(t48[:, 2 * w:2 * w + 2, :],
                                      bb[u % 2][:, 0:6 * C1].rearrange("p (t a n) -> p t n a", t=2, a=3),
                                      AX.X, ALU.add).then_inc(b_free[u % 2], 1)
                for w in range(2):
                    wait_used(dve, b_free, V_TOK + w, c, UB)
                cb.link(c, dve.scalar_tensor_tensor(out=t48[:, :, :], in0=t48[:, :, :], scalar=1.0 / XS,
                                                    in1=bias48[:, :].unsqueeze(1).broadcast_to([P, NT, C1]),
                                                    op0=ALU.mult, op1=ALU.add))

            def b_att(c):
                q, k = t48[:, :, 0:HD], t48[:, :, HD:2 * HD]
                full = [P, NT, HD, HD]
                dve.tensor_reduce(kext[:, 0, :], k, AX.X, ALU.max)
                cb.link(c, dve.tensor_reduce(kext[:, 1, :], k, AX.X, ALU.min))
                dve.tensor_tensor(m1[:, 0, :, :], q, kext[:, 0, :].unsqueeze(2).broadcast_to([P, NT, HD]), ALU.mult)
                cb.link(c, dve.tensor_tensor(m1[:, 1, :, :], q,
                                             kext[:, 1, :].unsqueeze(2).broadcast_to([P, NT, HD]), ALU.mult))
                dve.tensor_tensor(m1[:, 0, :, :], m1[:, 0, :, :], m1[:, 1, :, :], ALU.max)
                cb.link(c, dve.tensor_tensor(S, q.unsqueeze(3).broadcast_to(full), k.unsqueeze(2).broadcast_to(full),
                                             ALU.mult))
                dve.tensor_tensor(S, S, m1[:, 0, :, :].unsqueeze(3).broadcast_to(full), ALU.subtract)\
                   .then_inc(s_sd, 1)

            def b_att2(c):
                v = t48[:, :, 2 * HD:C1]
                full = [P, NT, HD, HD]
                dve.wait_ge(s_se, c + 1)
                cb.link(c, dve.tensor_reduce(den1[:, :, :], S, AX.X, ALU.add))
                cb.link(c, dve.tensor_tensor(S, S, v.unsqueeze(2).broadcast_to(full), ALU.mult))

            def b_att3(c):
                dve.tensor_reduce(o1[:, :, :], S, AX.X, ALU.add).then_inc(s_att1, 1)
                cb.link(c, dve.reciprocal(den1[:, :, :], den1[:, :, :]))
                dve.wait_ge(s_att1, c + 1)
                dve.tensor_tensor(o1[:, :, :], o1[:, :, :], den1[:, :, :], ALU.mult).then_inc(s_o1, 1)

            def b_up(c, i):
                ug = V_GU + 2 * i
                dve.wait_ge(s_sig, c * NI + i + 1)
                if i >= 2:
                    dve.wait_ge(s_hl, c * NI + i - 1)
                dve.scalar_tensor_tensor(out=hf[:, i % 2, :], in0=ebuf[:, i % 2, :], scalar=1.0,
                                         in1=bb[ug % 2][:, :], op0=ALU.add,
                                         op1=ALU.mult).then_inc(b_free[ug % 2], 1)

            def times_up(c, i):
                ug, uu = V_GU + 2 * i, V_GU + 2 * i + 1
                wait_used(dve, b_free, ug, c, UB)
                wait_full(dve, b_full, uu, c, UB)
                dve.scalar_tensor_tensor(out=hf[:, i % 2, :], in0=bb[uu % 2][:, :], scalar=sux[:, i:i + 1],
                                         in1=hf[:, i % 2, :], op0=ALU.mult, op1=ALU.mult)\
                   .then_inc(b_free[uu % 2], 1)

            def b_gate(c, i):
                if i:
                    times_up(c, i - 1)

            def b_half(c, t):
                if t == 0:
                    times_up(c, NI - 1)

            def b_down(c, t):
                u = V_DOWN + t
                wait_full(dve, b_full, u, c, UB)
                if t == 0:
                    dve.wait_ge(s_x1o, c + 1)
                if t:
                    dve.wait_ge(s_y, c * NT + t)
                dve.tensor_tensor(ytmp, bb[u % 2][:, :], dsb[:, :], ALU.mult).then_inc(b_free[u % 2], 1)
                wait_used(dve, b_free, u, c, UB)
                dve.tensor_tensor(x1[:, t, :], x1[:, t, :], ytmp, ALU.add).then_inc(s_y, 1)

            run(dve, {"a_ln": a_ln, "a_tok": a_tok, "a_q": a_q, "a_gate": a_gate, "a_max": a_max, "a_nm": a_nm,
                      "a_lo": a_lo, "a_pv": a_pv, "a_out": a_out, "a_ln1": a_ln1, "b_xT": b_xT, "b_tok": b_tok,
                      "b_att": b_att, "b_att2": b_att2, "b_att3": b_att3,
                      "b_gate": b_gate, "b_up": b_up, "b_half": b_half, "b_down": b_down}, (ca, cb))


def _parts(a, n=3):
    out, rest = [], np.asarray(a, np.float64)
    for _ in range(n):
        p = rest.astype(np.dtype("bfloat16"))
        out.append(p)
        rest = rest - p.astype(np.float64)
    return np.stack(out)


def _constants():
    bf = np.dtype("bfloat16")
    base = 2.0 ** (-2.0 ** (-(math.log2(NH) - 3)))
    slopes = (base ** np.arange(1, NH + 1, dtype=np.float64)).astype(np.float32).astype(np.float64)
    pos = np.arange(SEQ, dtype=np.float64)
    q_rows = np.zeros((6, NH, CHUNK), bf)
    q_rows[0:3] = _parts(slopes)[:, :, None]
    q_rows[3:6] = np.tile(_parts(-slopes[:, None] * pos[None, :]), (1, 1, NB))
    k_cols = np.ones((P, NT, ROWS - R_ALIBI), bf)
    for t in range(NT):
        k_cols[:, t, 0:3] = ((t % (SEQ // P)) * P + np.arange(P))[:, None]
    i = np.arange(P)
    return {
        "q_rows": q_rows,
        "k_cols": k_cols,
        "mask": np.where(i[None, :] > i[:, None], -1e30, 0.0).astype(bf),
        "ident_f": np.eye(P, dtype=np.float32), "ident_b": np.eye(P, dtype=bf),
        "tri": np.tile(np.tril(np.ones((NE, NE), np.float32), -1)[None], (P, 1, 1)),
    }


def kernel(**inputs):
    import concourse.bacc as _bacc
    from concourse.bass_utils import run_bass_kernel_spmd as _run

    a = {k: np.asarray(v) for k, v in inputs.items()}
    laid = {
        "x": a["L0_attn_hidden_states"].reshape(BATCH * SEQ, HID),
        "wqkv": a["L0_attn_Wqkv"], "wo": a["L0_attn_Wo"],
        "lora_a": a["L0_ffn_A"].reshape(NE * LR, HID).T,
        "lora_b": a["L0_ffn_B"].transpose(0, 2, 1).reshape(NE * LR, HID),
        "wr": a["L0_ffn_Wr"].T,
        "wq1": a["L1_attn_Wq"], "bq1": a["L1_attn_bq"],
        "wk1": a["L1_attn_Wk"].reshape(HID, HD), "bk1": a["L1_attn_bk"].reshape(HD),
        "wv1": a["L1_attn_Wv"].reshape(HID, HD), "bv1": a["L1_attn_bv"].reshape(HD),
        "gate_w": a["L1_ffn_gate_wq"].T, "gate_s": a["L1_ffn_gate_scale"].reshape(NI, P).T,
        "up_w": a["L1_ffn_up_wq"].T, "up_s": a["L1_ffn_up_scale"].reshape(NI, P).T,
        "down_w": a["L1_ffn_down_wq"].T.reshape(NI, P, HID).transpose(1, 0, 2).reshape(P, NI * HID),
        "down_s": a["L1_ffn_down_scale"],
    }
    laid.update(_constants())

    nc = _bacc.Bacc("TRN2", target_bir_lowering=False, num_devices=1)
    arrays, args = {}, []
    for name, v in laid.items():
        v = np.ascontiguousarray(v)
        arrays[f"in_{name}"] = v
        args.append(nc.dram_tensor(f"in_{name}", v.shape, mybir.dt.from_np(v.dtype), kind="ExternalInput").ap())
    args.append(nc.dram_tensor("out_y", (BATCH * SEQ, HID), F32, kind="ExternalOutput").ap())
    build(nc, *args)
    r = _run(nc, [arrays], core_ids=[0])
    return r.results[0]["out_y"].reshape(BATCH, SEQ, HID)
```
